# Optimizing a Trainium2 kernel written in Bass

```python
import numpy as np
import jax
import jax.numpy as jnp

def _softmax(x, axis=-1):
    return jax.nn.softmax(x, axis=axis)

def _gelu(x):
    return jax.nn.gelu(x, approximate=True)

def _silu(x):
    return jax.nn.silu(x)

def _sigmoid(x):
    return jax.nn.sigmoid(x)

def _layernorm(x, axis=-1, eps=1e-05):
    m = jnp.mean(x, axis=axis, keepdims=True)
    v = jnp.var(x, axis=axis, keepdims=True)
    return (x - m) / jnp.sqrt(v + eps)

def _scatter_add(tgt, idx, src, axis=0):
    return tgt.at[idx].add(src)

def _segment_sum(src, seg, n):
    return jax.ops.segment_sum(src, seg, n)
kernel_name = 'mk_gnn_ffn_d1_gnn_r32_0053bd'

def setup_inputs(seed: int=0):
    np.random.seed(seed)
    _w = jnp.asarray

    def _rec_inputs():
        import jax
        import jax.numpy as jnp
        _gk = jax.random.key(seed)
        x = -6.415e-05 + 1 * jax.random.normal(jax.random.fold_in(_gk, 1), (625, 512), jnp.float32)
        src = jax.random.randint(jax.random.fold_in(_gk, 2), (20000,), 0, 625, jnp.int32)
        dst = jax.random.randint(jax.random.fold_in(_gk, 3), (20000,), 0, 625, jnp.int32)
        _o = jnp.argsort(dst, stable=True)
        src = src[_o]
        dst = dst[_o]
        edge_type_8 = jax.random.randint(jax.random.fold_in(_gk, 12), (20000,), 0, 8, jnp.int32)
        return (x, src, dst, edge_type_8)
    x, src, dst, edge_type_8 = _rec_inputs()

    def _L0_gnn_setup():
        import jax, jax.numpy as jnp
        import numpy as np
        N = 625
        E = 5000
        D = 512
        R = 8
        key = jax.random.key(seed)
        ks = jax.random.split(key, 8)
        inp = {'input': jax.random.normal(ks[0], (N, D), dtype=jnp.float32), 'heads': jax.random.randint(ks[1], (E,), 0, N), 'tails': jax.random.randint(ks[2], (E,), 0, N), 'rel': jax.random.randint(ks[3], (E,), 0, R), 'W_self': jax.random.normal(ks[4], (D, D), dtype=jnp.float32) * 0.03, 'b_self': jnp.zeros((D,), dtype=jnp.float32), 'W_rel': jax.random.normal(ks[5], (2 * R, D, D), dtype=jnp.float32) * 0.03, 'b_rel': jnp.zeros((2 * R, D), dtype=jnp.float32)}
        return inp
    _L0_gnn_all = _L0_gnn_setup()
    _L0_gnn_in = {k: v for k, v in _L0_gnn_all.items() if k in ('W_self', 'b_self', 'W_rel', 'b_rel')}
    del _L0_gnn_all

    def _L0_ffn_setup():
        import jax, jax.numpy as jnp
        import numpy as np
        TOP_K = 2
        key = jax.random.key(seed)
        ks = jax.random.split(key, 4)
        b, t, d, e, h = (2, 64, 512, 8, 1024)
        scale = 0.02
        return {'x': jax.random.normal(ks[0], (b, t, d), dtype=jnp.float32), 'router_w': jax.random.normal(ks[1], (e, d), dtype=jnp.float32) * scale, 'router_b': jnp.zeros((e,), dtype=jnp.float32), 'fc1_w': jax.random.normal(ks[2], (e, 2 * h, d), dtype=jnp.float32) * scale, 'fc1_b': jnp.zeros((e, 2 * h), dtype=jnp.float32), 'fc2_w': jax.random.normal(ks[3], (e, d, h), dtype=jnp.float32) * scale, 'fc2_b': jnp.zeros((e, d), dtype=jnp.float32)}
    _L0_ffn_all = _L0_ffn_setup()
    _L0_ffn_in = {k: v for k, v in _L0_ffn_all.items() if k in ('router_w', 'router_b', 'fc1_w', 'fc1_b', 'fc2_w', 'fc2_b')}
    del _L0_ffn_all
    return {'x': x, 'src': src, 'dst': dst, 'edge_type_8': edge_type_8, 'L0_gnn_W_self': _L0_gnn_in['W_self'], 'L0_gnn_b_self': _L0_gnn_in['b_self'], 'L0_gnn_W_rel': _L0_gnn_in['W_rel'], 'L0_gnn_b_rel': _L0_gnn_in['b_rel'], 'L0_ffn_router_w': _L0_ffn_in['router_w'], 'L0_ffn_router_b': _L0_ffn_in['router_b'], 'L0_ffn_fc1_w': _L0_ffn_in['fc1_w'], 'L0_ffn_fc1_b': _L0_ffn_in['fc1_b'], 'L0_ffn_fc2_w': _L0_ffn_in['fc2_w'], 'L0_ffn_fc2_b': _L0_ffn_in['fc2_b']}

def reference(x, src, dst, edge_type_8, L0_gnn_W_self, L0_gnn_b_self, L0_gnn_W_rel, L0_gnn_b_rel, L0_ffn_router_w, L0_ffn_router_b, L0_ffn_fc1_w, L0_ffn_fc1_b, L0_ffn_fc2_w, L0_ffn_fc2_b):
    import jax
    import jax.numpy as jnp

    def _L0_gnn_ref(input, heads, tails, rel, W_self, b_self, W_rel, b_rel):
        import jax, jax.numpy as jnp
        import numpy as np
        N = 625
        E = 5000
        D = 512
        R = 8
        h_self = input @ W_self.T + b_self
        H_all = jnp.einsum('rod,nd->rno', W_rel, input) + b_rel[:, None, :]
        msg_to_heads = H_all[rel, tails]
        msg_to_tails = H_all[rel + R, heads]
        agg = jax.ops.segment_sum(msg_to_heads, heads, num_segments=N) + jax.ops.segment_sum(msg_to_tails, tails, num_segments=N)
        return jax.nn.relu(h_self + agg)

    def _L0_ffn_ref(x, router_w, router_b, fc1_w, fc1_b, fc2_w, fc2_b):
        import jax, jax.numpy as jnp
        import numpy as np
        TOP_K = 2
        n_experts = router_w.shape[0]
        temp = 1.0
        logits = (jnp.einsum('btd,ed->bte', x, router_w) + router_b) / temp
        topk_val, topk_idx = jax.lax.top_k(logits, TOP_K)
        weights = jax.nn.softmax(topk_val, axis=-1)
        onehot = jax.nn.one_hot(topk_idx, n_experts, dtype=x.dtype)
        cw = jnp.einsum('btk,btke->bte', weights, onehot)
        h = jnp.einsum('btd,efd->btef', x, fc1_w) + fc1_b
        h1, h2 = jnp.split(h, 2, axis=-1)
        a = jax.nn.silu(h1) * h2
        y = jnp.einsum('bteh,edh->bted', a, fc2_w) + fc2_b
        out = jnp.einsum('bted,bte->btd', y, cw)
        return out
    x = x + _L0_gnn_ref(_layernorm(x, axis=-1), src, dst, edge_type_8, L0_gnn_W_self, L0_gnn_b_self, L0_gnn_W_rel, L0_gnn_b_rel)
    x = x + _L0_ffn_ref(_layernorm(x, axis=-1)[None], L0_ffn_router_w, L0_ffn_router_b, L0_ffn_fc1_w, L0_ffn_fc1_b, L0_ffn_fc2_w, L0_ffn_fc2_b)[0]
    return x

_drawn_inputs = setup_inputs


def setup_inputs(seed=0):
    import zlib

    import numpy as np

    out = dict(_drawn_inputs(seed))
    spreads = {'L0_gnn_b_self': (0.0, 0.448),
     'L0_gnn_b_rel': (0.0, 0.1),
     'L0_ffn_router_b': (0.0, 0.8),
     'L0_ffn_fc1_b': (0.0, 0.8),
     'L0_ffn_fc2_b': (0.0, 0.467)}
    factors = {'L0_ffn_router_w': 3.222, 'L0_ffn_fc1_w': 4.455, 'L0_ffn_fc2_w': 4.466}
    for name, (base, spread) in spreads.items():
        noise = np.random.default_rng([zlib.crc32(name.encode()), seed]).standard_normal(out[name].shape)
        drawn = base * np.exp(spread * noise) if base else spread * noise
        out[name] = jnp.asarray(drawn.astype(out[name].dtype))
    for name, factor in factors.items():
        out[name] = (out[name] * factor).astype(out[name].dtype)
    return out
```

```python
from contextlib import ExitStack

import concourse.bass as bass
from concourse import mybir

F32 = mybir.dt.float32
F16 = mybir.dt.float16
I32 = mybir.dt.int32
U32 = mybir.dt.uint32
ACT = mybir.ActivationFunctionType
ALU = mybir.AluOpType
AX_X = mybir.AxisListType.X

P = 128
NODES = 625
D = 512
KD = D // P
NT = (NODES + P - 1) // P
PADDED = NT * P
LAST = NODES - (NT - 1) * P
EDGES = 20000
RELS = 8
EXPERTS = 8
HID = 1024
KH = HID // P

EP = 125
EC = EDGES // EP
EDGE_CHUNKS = (EDGES + NT * (P - 1)) // P
COLS_PER_REL = EC // RELS
COLS_PER_TILE = COLS_PER_REL // NT
RING = 20
HALF = RING // 2
SEG = 2 * COLS_PER_REL
TAIL = EDGE_CHUNKS - 4 * SEG
assert TAIL == 1 and SEG == 2 * RING

CH = 1024
REL_CHUNKS = 2
GNN_CHUNKS = REL_CHUNKS * (2 * RELS + 1)
SLOTS = 12
RAW = 4
TOK = 313

SX = 64.0
SW = 64.0
SH = 64.0
SA = 16.0
LN_EPS = 1e-5


def fc1_order(j):
    return 2 * j + 1 if j < 4 else 4 + j


def build(nc, x, src, dst, rel, gnn_w, b_self, b_rel, router_w, router_b, ffn_w, fc1_b, fc2_b, out):
    with ExitStack() as ctx:
        def sb(name, shape, dt):
            return ctx.enter_context(nc.sbuf_tensor(name, shape, dt))

        def sem(name):
            return ctx.enter_context(nc.semaphore(name))

        x_sb = sb("x_sb", [P, NT, D], F32)
        xT_hi = sb("xT_hi", [P, KD, PADDED], F16)
        xT_lo = sb("xT_lo", [P, KD, PADDED], F16)
        w_raw = sb("w_raw", [P, RAW, CH], F32)
        w_hi = sb("w_hi", [P, SLOTS, CH], F16)
        w_lo = sb("w_lo", [P, SLOTS, CH], F16)

        def self_sb(t):
            return (w_hi[:, KH + t, :] if t < 4 else w_lo[:, KH, :]).bitcast(F32)

        scratch = sb("scratch", [P, 2 * NT * 1024 + (RING + 1) * 1024 + 20 * 456 + (SEG + 1) * P], F16)
        cut = [0]

        def part(cols):
            cut[0] += cols
            return scratch[:, cut[0] - cols:cut[0]]

        rows_out = part(2 * NT * 1024).rearrange("p (q t c) -> p q t c", q=2, t=NT)
        gathered = part((RING + 1) * 1024).rearrange("p (s c) -> p s c", c=1024)
        sort_hot = part(20 * 456).rearrange("p (s c) -> p s c", c=456)
        dest_hot = part((SEG + 1) * P).rearrange("p (s c) -> p s c", c=P)
        cut[0] = 2 * NT * 1024

        def edge_part(rows, dt):
            return part(2 * rows * EC).bitcast(dt).rearrange("p (n c) -> p n c", c=EC)

        edge_in = edge_part(3, I32)
        edge_t = edge_part(2, I32)
        edge_l = edge_part(2, I32)
        tile_f = edge_part(2, F32)
        place = edge_part(2, F32)
        place_i = edge_part(2, I32)
        lo_i = edge_part(2, I32)
        rel_f = edge_part(1, F32)[:, 0, :]
        in_bucket = edge_part(2 * NT, F32).rearrange("p (l b) c -> p l b c", l=2)
        running = edge_part(2 * NT, F32).rearrange("p (l b) c -> p l b c", l=2)
        assert cut[0] <= 2 * NT * 1024 + (RING + 1) * 1024
        cut[0] = 0
        aT_hi = part(KH * PADDED).rearrange("p (k n) -> p k n", n=PADDED)
        aT_lo = part(KH * PADDED).rearrange("p (k n) -> p k n", n=PADDED)
        acc = part(2 * NT * D).bitcast(F32).rearrange("p (t n) -> p t n", t=NT)
        silu = part(2 * 2 * 320).bitcast(F32).rearrange("p (c n) -> p c n", c=2)
        glu = part(2 * 2 * 320).bitcast(F32).rearrange("p (c n) -> p c n", c=2)
        cwT = part(2 * PADDED).bitcast(F32)[0:EXPERTS, :]

        xn = sb("xn", [P, 2, D], F32)
        bias_row = sb("bias_row", [P, 2, D], F32)
        b_self_row = sb("b_self_row", [P, D], F32)
        ident = sb("ident", [P, P], F32)
        zeros = sb("zeros", [P, D], F16)
        iota_f = sb("iota_f", [P, 176], F32)
        iota_h = sb("iota_h", [P, 176], F16)
        iota_i = sb("iota_i", [P, 176], I32)
        before = sb("before", [P, P], F32)
        ones = sb("ones", [P, EC], F32)
        stats = sb("stats", [P, NT, 6], F32)
        mv = sb("mv", [P, NT, 2], F32)
        rstd = sb("rstd", [P, NT], F32)
        std = sb("std", [P, NT], F32)
        node_f = sb("node_f", [P, 2, EC], F32)
        code_f = sb("code_f", [P, 2, EC], F32)
        part_sum = sb("part_sum", [P, 2, NT], F32)
        pad_i = sb("pad_i", [P, 2, NT], I32)
        pad_f = sb("pad_f", [P, 2, NT], F32)
        pad_end = sb("pad_end", [P, 2, NT], F32)
        pad_base = sb("pad_base", [P, 2, NT], F32)
        offset = sb("offset", [P, 2, NT], F32)
        pos_lo = sb("pos_lo", [P, 2 * EC], F32)
        pos_hi = sb("pos_hi", [P, 2 * EC], F32)
        bank_f = sb("bank_f", [1, 2, EDGE_CHUNKS], F32)
        bank_i = sb("bank_i", [1, 2, EDGE_CHUNKS], I32)
        code_i = sb("code_i", [P, EDGE_CHUNKS], I32)
        part_i = sb("part_i", [P, 2, EDGE_CHUNKS], I32)
        dest_f = sb("dest_f", [P, 2, EDGE_CHUNKS], F32)
        row_f = sb("row_f", [P, EDGE_CHUNKS], F32)
        row_rel = sb("row_rel", [P, EDGE_CHUNKS], F32)
        row_idx = sb("row_idx", [P, 2, EDGE_CHUNKS], U32)
        ring_idx = sb("ring_idx", [P, RING + 1], U32)
        rw_raw = sb("rw_raw", [P, KD * EXPERTS], F32)
        rw_hi = sb("rw_hi", [P, KD * EXPERTS], F16)
        rw_lo = sb("rw_lo", [P, KD * EXPERTS], F16)
        rb_row = sb("rb_row", [P, EXPERTS], F32)
        logits = sb("logits", [P, NT, EXPERTS], F32)
        top = sb("top", [P, NT, 8], F32)
        top_i = sb("top_i", [P, NT, 8], U32)
        top_if = sb("top_if", [P, NT, 8], F32)
        soft = sb("soft", [P, 4, NT], F32)
        cw_a = sb("cw_a", [P, EXPERTS, NT], F32)
        cw_b = sb("cw_b", [P, EXPERTS, NT], F32)
        cw = sb("cw", [P, NT, EXPERTS], F32)
        cw_s = sb("cw_s", [P, EXPERTS * NT], F32)
        b1 = sb("b1", [P, EXPERTS * 2 * KH], F32)
        b1_s = sb("b1_s", [P, EXPERTS * 2 * KH], F32)
        b2 = sb("b2", [EXPERTS, D], F32)
        ps = ctx.enter_context(nc.psum_tensor("ps", [P, 8, 512], F32))
        ps_flat = ps[:, :, :].rearrange("p b n -> p (b n)")
        rows_dram = nc.dram_tensor("rows_dram", [2 * RELS * PADDED, 2 * D], F16, kind="Internal").ap()
        rows_by_rel = rows_dram.rearrange("(r t p) c -> p r t c", p=P, t=NT)

        s_x = sem("x_loaded")
        s_xpad = sem("x_pad_zeroed")
        s_edges = sem("edges_loaded")
        s_small = sem("small_loaded")
        s_bias = [sem(f"bias_loaded{q}") for q in range(2)]
        s_raw = [sem(f"w_raw_loaded{s}") for s in range(RAW)]
        s_const = sem("consts_ready")
        s_pool = sem("pool_chain")
        s_dve = sem("dve_chain")
        s_var = sem("var_ready")
        s_std = sem("std_ready")
        s_xn = sem("xn_ready")
        s_xT = sem("xn_transposed")
        s_xhi = sem("xT_hi_ready")
        s_xlo = sem("xT_lo_ready")
        s_whi = sem("w_hi_ready")
        s_wlo = sem("w_lo_ready")
        s_sum = sem("part_sum_ready")
        s_pre = sem("prefix_done")
        s_bank = sem("bank_table_ready")
        s_hot = sem("sort_hot_ready")
        s_sorted = sem("column_sorted")
        s_dec = sem("list_decoded")
        s_tr = sem("transformed")
        s_row = sem("row_biased")
        s_rhi = sem("row_hi_ready")
        s_rlo = sem("row_lo_ready")
        s_store = [sem(f"rows_stored{q}") for q in range(2)]
        s_idx = sem("idx_copied")
        s_gat = [sem(f"gathered{s}") for s in range(RING + 1)]
        s_dhot = sem("dest_hot_ready")
        s_seg = sem("chunk_summed")
        s_zero = sem("sums_zeroed")
        s_self = sem("self_evacuated")
        s_gnn = sem("gnn_out_ready")
        s_lg = sem("logits_ready")
        s_dif = sem("top_diff_ready")
        s_exp = sem("top_exp_ready")
        s_cw = sem("cw_ready")
        s_cwt = sem("cw_transposed")
        s_cwc = sem("cwT_copied")
        s_b2 = sem("bias2_summed")
        s_fc1 = sem("fc1_done")
        s_silu = sem("silu_ready")
        s_turn = sem("silu_turn")
        s_free1 = sem("fc1_pair_free")
        s_ahi = sem("a_hi_ready")
        s_alo = sem("a_lo_ready")
        s_fc2 = sem("fc2_done")
        s_comb = sem("combined")
        s_rwh = sem("router_hi_ready")
        s_rwl = sem("router_lo_ready")
        s_out = sem("out_stored")

        block = ctx.enter_context(nc.Block())

        @block.sync
        def _(sp):
            for n, a in enumerate((src, dst, rel)):
                sp.dma_start(edge_in[0:EP, n, :], a.rearrange("(p c) -> p c", c=EC)).then_inc(s_edges, 16)
            sp.dma_start(x_sb[:, 0:NT - 1, :],
                         x[0:(NT - 1) * P, :].rearrange("(t p) d -> p t d", p=P)).then_inc(s_x, 16)
            sp.wait_ge(s_xpad, 1)
            sp.dma_start(x_sb[0:LAST - 1, NT - 1, :], x[(NT - 1) * P:NODES - 1, :]).then_inc(s_x, 16)
            sp.dma_start(x_sb[LAST - 1:LAST, NT - 1, :], x[NODES - 1:NODES, :]).then_inc(s_x, 16)

            def load_gnn(chunk, slot):
                sp.dma_start(w_raw[:, slot, :], gnn_w[bass.ds(chunk, 1), :, :].rearrange("a p c -> p (a c)"))\
                    .then_inc(s_raw[slot], 16)

            def load_bias(r, q):
                sp.dma_start(bias_row[:, q, :], b_rel[bass.ds(r, 1), :].to_broadcast([P, D]))\
                    .then_inc(s_bias[q], 16)

            load_gnn(0, 0)
            load_gnn(1, 1)
            load_bias(0, 0)
            sp.dma_start(b_self_row[:, :], b_self.to_broadcast([P, D])).then_inc(s_small, 16)
            sp.dma_start(rw_raw[:, :], router_w).then_inc(s_small, 16)
            sp.dma_start(rb_row[:, :], router_b.to_broadcast([P, EXPERTS])).then_inc(s_small, 16)
            sp.dma_start(b1[:, :], fc1_b).then_inc(s_small, 16)
            sp.dma_start(b2[:, :], fc2_b).then_inc(s_small, 16)

            def relation(r, q, first, last):
                sp.wait_ge(s_wlo, 2 * r + 2)
                load_gnn(2 * r + 2, 2 * (1 - q))
                load_gnn(2 * r + 3, 2 * (1 - q) + 1)
                if not last:
                    if not first:
                        sp.wait_ge(s_row, NT * r)
                    load_bias(r + 1, 1 - q)
                sp.wait_ge(s_rlo, NT * (r + 1))
                sp.dma_start(rows_by_rel[:, bass.ds(r, 1), :, :].rearrange("p r t c -> p (r t) c"),
                             rows_out[:, q, :, :]).then_inc(s_store[q], 16)

            relation(0, 0, True, False)
            relation(1, 1, False, False)
            with sp.Fori(1, RELS - 1) as i:
                relation(2 * i, 0, False, False)
                relation(2 * i + 1, 1, False, False)
            relation(2 * RELS - 2, 0, False, False)
            relation(2 * RELS - 1, 1, False, True)

            with sp.Fori(0, EXPERTS * SLOTS // RAW) as i:
                for s in range(RAW):
                    sp.wait_ge(s_wlo, GNN_CHUNKS - RAW + RAW * i + s + 1)
                    sp.dma_start(w_raw[:, s, :],
                                 ffn_w[bass.ds(RAW * i + s, 1), :, :].rearrange("a p c -> p (a c)"))\
                        .then_inc(s_raw[s], 16)
            for t in range(NT):
                sp.wait_ge(s_comb, NT * EXPERTS + t + 1)
                if t < NT - 1:
                    sp.dma_start(out[t * P:(t + 1) * P, :], acc[:, t, :]).then_inc(s_out, 16)
                else:
                    sp.dma_start(out[t * P:NODES - 1, :], acc[0:LAST - 1, t, :]).then_inc(s_out, 16)
                    sp.dma_start(out[NODES - 1:NODES, :], acc[LAST - 1:LAST, t, :]).then_inc(s_out, 16)
            sp.wait_ge(s_store[0], 16 * RELS)
            sp.wait_ge(s_store[1], 16 * RELS)
            sp.wait_ge(s_out, 16 * (NT + 1))

        @block.gpsimd
        def _(pool):
            links = [0]

            def link(ins):
                links[0] += 1
                ins.then_inc(s_pool, 1)
                pool.wait_ge(s_pool, links[0])

            link(pool.memset(ident[:, :], 0.0))
            pool.affine_select(out=ident[:, :], in_=ident[:, :], compare_op=ALU.not_equal, fill=1.0, base=0,
                               pattern=[[-1, P]], channel_multiplier=1).then_inc(s_const, 1)
            link(pool.memset(before[:, :], 0.0))
            pool.affine_select(out=before[:, :], in_=before[:, :], compare_op=ALU.is_ge, fill=1.0, base=0,
                               pattern=[[-1, P]], channel_multiplier=1).then_inc(s_const, 1)
            link(pool.iota(iota_i[:, :], pattern=[[1, 176]], base=0, channel_multiplier=0))
            link(pool.tensor_copy(iota_f[:, :], iota_i[:, :]))
            pool.tensor_copy(iota_h[:, :], iota_f[:, :]).then_inc(s_const, 1)
            pool.memset(zeros[:, :], 0.0).then_inc(s_const, 1)
            pool.memset(ones[:, :], 1.0).then_inc(s_const, 1)

            def gather(l, slot):
                pool.indirect_dma_start(gathered[:, slot, :], None, rows_dram[0:(l + 1) * RELS * PADDED, :],
                                        bass.IndirectOffsetOnAxis(ap=ring_idx[:, slot:slot + 1], axis=0))\
                    .then_inc(s_gat[slot], 16)

            def gather_half(l, a, h, batch, summed):
                if summed is not None:
                    pool.wait_ge(s_seg, summed)
                    pool.sem_inc(s_idx, 1)
                at = l * EDGE_CHUNKS + RING * a + HALF * h
                pool.tensor_copy(ring_idx[:, HALF * h:HALF * h + HALF],
                                 row_idx[:, :, :].rearrange("p l c -> p (l c)")[:, bass.ds(at, HALF)])\
                    .then_inc(s_idx, 1)
                pool.wait_ge(s_idx, batch)
                pool.sem_inc(s_pool, 1)
                for s in range(HALF * h, HALF * h + HALF):
                    gather(l, s)

            turns = EDGE_CHUNKS // RING
            for l in range(2):
                pool.wait_ge(s_dec, l + 1)
                for q in range(2):
                    pool.wait_ge(s_store[q], 16 * (RELS // 2) * (l + 1))
                base = l * (4 * turns - 2 + 1)
                for h in range(2):
                    gather_half(l, 0, h, base + (h + 1) * (1 + l), None if l == 0 else
                                EDGE_CHUNKS - TAIL - RING + HALF * (h + 1))
                first = base + 2 * (1 + l)
                with pool.Fori(1, turns) as a:
                    for h in range(2):
                        gather_half(l, a, h, 4 * a + (first - 4 + 2 * (h + 1)),
                                    RING * a + (l * EDGE_CHUNKS - RING + HALF * (h + 1)))
                if l == 1:
                    pool.wait_ge(s_seg, EDGE_CHUNKS)
                pool.tensor_copy(ring_idx[:, RING:RING + 1],
                                 row_idx[:, l, EDGE_CHUNKS - 1:EDGE_CHUNKS]).then_inc(s_idx, 1)
                pool.wait_ge(s_idx, first + 4 * (turns - 1) + 1)
                gather(l, RING)

        @block.scalar
        def _(act):
            def split_hi(slot, raw, loaded):
                act.wait_ge(s_raw[raw], loaded)
                act.activation(w_hi[:, slot, :], w_raw[:, raw, :], ACT.Copy, scale=SW).then_inc(s_whi, 1)

            def layer_norm_part(n):
                act.wait_ge(s_var, n + 1)
                act.activation(std[:, :], rstd[:, :], ACT.Sqrt).then_inc(s_std, 1)
                for t in range(NT):
                    act.wait_ge(s_xT, NT * n + t + 1)
                    act.activation(xT_hi[:, :, t * P:(t + 1) * P],
                                   ps[:, 5 + t % 2, :].rearrange("p (k m) -> p k m", k=KD),
                                   ACT.Copy, scale=SX).then_inc(s_xhi, 1)

            layer_norm_part(0)
            split_hi(0, 0, 16)
            split_hi(1, 1, 16)
            act.wait_ge(s_small, 16 * 5)
            act.activation(rw_hi[:, :], rw_raw[:, :], ACT.Copy, scale=SW).then_inc(s_rwh, 1)

            def relation(r, q, i):
                for t in range(NT):
                    if t < 2:
                        slot = 2 * (1 - q) + t
                        if t == 0 and not (isinstance(r, int) and r == 0):
                            act.wait_ge(s_tr, NT * r)
                        split_hi(slot, slot, 16 * (i + 1) + 16 * q)
                    act.wait_ge(s_row, NT * r + t + 1)
                    act.activation(rows_out[:, q, t, 0:D], xn[:, t % 2, :], ACT.Copy, scale=SH)\
                        .then_inc(s_rhi, 1)

            relation(0, 0, 0)
            relation(1, 1, 0)
            with act.Fori(1, RELS) as i:
                relation(2 * i, 0, i)
                relation(2 * i + 1, 1, i)
            for t in range(NT):
                act.wait_ge(s_tr, 2 * RELS * NT + t + 1)
                act.activation(self_sb(t), ps[:, 5 + t % 2, :], ACT.Copy, scale=1.0 / (SX * SW))\
                    .then_inc(s_self, 1)

            def split_ffn(slot, n):
                raw = n[1]
                used = GNN_CHUNKS // RAW + (1 if raw < GNN_CHUNKS % RAW else 0)
                split_hi(slot, raw, 16 * (n[0] + used + 1))

            for j in range(KH):
                split_ffn(j, (j // RAW, j % RAW))
            layer_norm_part(1)
            act.wait_ge(s_dif, 1)
            act.activation(soft[:, 1, :], soft[:, 0, :], ACT.Exp).then_inc(s_exp, 1)

            def expert(e, last):
                for j in range(KH):
                    for c in range(2):
                        act.wait_ge(s_fc1, 16 * e + 2 * j + c + 1)
                        act.sem_inc(s_turn, 1)
                        act.activation(silu[:, c, 0:TOK], ps[:, 2 * c, 0:TOK], ACT.Silu,
                                       bias=b1[:, bass.ds(2 * KH * e + j, 1)], scale=1.0 / (SX * SW))\
                            .then_inc(s_silu, 1)
                        act.wait_ge(s_free1, 16 * e + 2 * j + c + 3)
                        act.activation(aT_hi[:, j, c * TOK:(c + 1) * TOK], glu[:, c, 0:TOK], ACT.Copy,
                                       scale=SA / (SX * SW)).then_inc(s_ahi, 1)
                    if j < 4:
                        n = KH + (j if last else 2 * j)
                        split_ffn(KH + j, (3 * e + n // RAW, n % RAW))
                    if not last:
                        n = KH + fc1_order(j)
                        split_ffn(j, (3 * e + n // RAW, n % RAW))

            with act.Fori(0, EXPERTS - 1) as e:
                expert(e, False)
            last_expert(expert)

        @block.vector
        def _(dve):
            links = [0]

            def link(ins):
                links[0] += 1
                ins.then_inc(s_dve, 1)
                dve.wait_ge(s_dve, links[0])

            def split_lo(slot, raw, hi_count):
                dve.wait_ge(s_whi, hi_count)
                dve.scalar_tensor_tensor(out=w_lo[:, slot, :], in0=w_raw[:, raw, :], scalar=SW,
                                         in1=w_hi[:, slot, :], op0=ALU.mult, op1=ALU.subtract)\
                    .then_inc(s_wlo, 1)

            def layer_norm_part(n):
                for t in range(NT):
                    if n == 0:
                        if t == 0:
                            dve.wait_ge(s_x, 48)
                    ins = dve.bn_stats(stats[:, t, :], x_sb[:, t, :])
                link(ins)
                for t in range(NT):
                    ins = dve.bn_aggr(mv[:, t, :], stats[:, t, :])
                link(ins)
                dve.tensor_scalar(rstd[:, :], mv[:, :, 1], LN_EPS, None, ALU.add).then_inc(s_var, 1)
                dve.wait_ge(s_std, n + 1)
                link(dve.reciprocal(rstd[:, :], std[:, :]))

                def normalise(t):
                    if t >= 2:
                        dve.wait_ge(s_xT, NT * n + t - 1)
                    dve.tensor_scalar(xn[:, t % 2, :], x_sb[:, t, :], mv[:, t, 0:1], rstd[:, t:t + 1],
                                      ALU.subtract, ALU.mult).then_inc(s_xn, 1)

                def low(t):
                    dve.wait_ge(s_xhi, NT * n + t + 1)
                    dve.scalar_tensor_tensor(
                        out=xT_lo[:, :, t * P:(t + 1) * P],
                        in0=ps[:, 5 + t % 2, :].rearrange("p (k m) -> p k m", k=KD), scalar=SX,
                        in1=xT_hi[:, :, t * P:(t + 1) * P], op0=ALU.mult, op1=ALU.subtract)\
                        .then_inc(s_xlo, 1)

                for t in range(NT):
                    normalise(t)
                    if t >= 1:
                        low(t - 1)
                low(NT - 1)

            dve.memset(x_sb[96:P, NT - 1, :], 0.0).then_inc(s_xpad, 1)
            layer_norm_part(0)
            split_lo(0, 0, 1)
            split_lo(1, 1, 2)

            E = slice(0, EP)
            dve.wait_ge(s_edges, 48)
            dve.wait_ge(s_const, 5)
            dve.tensor_scalar(edge_t[E, :, :], edge_in[E, 0:2, :], 7, None, ALU.logical_shift_right)
            link(dve.tensor_scalar(edge_l[E, :, :], edge_in[E, 0:2, :], P - 1, None, ALU.bitwise_and))
            dve.tensor_copy(tile_f[E, :, :], edge_t[E, :, :])
            dve.tensor_copy(place[E, :, :], edge_l[E, :, :])
            dve.tensor_copy(node_f[E, 0, :], edge_in[E, 1, :])
            dve.tensor_copy(node_f[E, 1, :], edge_in[E, 0, :])
            link(dve.tensor_copy(rel_f[E, :], edge_in[E, 2, :]))
            link(dve.tensor_scalar(rel_f[E, :], rel_f[E, :], 256.0, 1.0, ALU.mult, ALU.add))
            for l in range(2):
                dve.tensor_tensor(code_f[E, l, :], place[E, l, :], rel_f[E, :], ALU.add)
            for l in range(2):
                for b in range(NT):
                    ins = dve.tensor_scalar(in_bucket[E, l, b, :], tile_f[E, l, :], float(b), None, ALU.is_equal)
            link(ins)
            for l in range(2):
                for b in range(NT):
                    ins = dve.tensor_tensor_scan(running[E, l, b, :], ones[E, :], in_bucket[E, l, b, :], 0.0,
                                                 ALU.mult, ALU.add)
            link(ins)
            dve.tensor_copy(part_sum[E, :, :], running[E, :, :, EC - 1]).then_inc(s_sum, 1)
            dve.wait_ge(s_pre, 1)
            early = ps[:, 7, 0:2 * NT].rearrange("p (l b) -> p l b", l=2)
            total = ps[:, 7, 16:16 + 2 * NT].rearrange("p (l b) -> p l b", l=2)
            link(dve.tensor_scalar(pad_f[:, :, :], total, float(P - 1), None, ALU.add))
            link(dve.tensor_copy(pad_i[:, :, :], pad_f[:, :, :]))
            link(dve.tensor_scalar(pad_i[:, :, :], pad_i[:, :, :], -P, None, ALU.bitwise_and))
            link(dve.tensor_copy(pad_f[:, :, :], pad_i[:, :, :]))
            for l in range(2):
                ins = dve.tensor_tensor_scan(pad_end[:, l, :], ones[:, 0:NT], pad_f[:, l, :], 0.0, ALU.mult, ALU.add)
            link(ins)
            link(dve.tensor_tensor(pad_base[:, :, :], pad_end[:, :, :], pad_f[:, :, :], ALU.subtract))
            link(dve.scalar_tensor_tensor(out=offset[E, :, :], in0=pad_base[E, :, :], scalar=-1.0,
                                          in1=early[E, :, :], op0=ALU.add, op1=ALU.add))
            for l in range(2):
                for b in range(NT):
                    ins = dve.scalar_tensor_tensor(out=running[E, l, b, :], in0=running[E, l, b, :],
                                                   scalar=offset[E, l, b:b + 1], in1=in_bucket[E, l, b, :],
                                                   op0=ALU.add, op1=ALU.mult)
            link(ins)
            link(dve.tensor_tensor(place[E, :, :], running[E, :, 0, :], running[E, :, 1, :], ALU.add))
            for b in range(2, NT):
                link(dve.tensor_tensor(place[E, :, :], place[E, :, :], running[E, :, b, :], ALU.add))
            link(dve.tensor_copy(place_i[E, :, :], place[E, :, :]))
            dve.tensor_scalar(lo_i[E, :, :], place_i[E, :, :], P - 1, None, ALU.bitwise_and)
            link(dve.tensor_scalar(edge_t[E, :, :], place_i[E, :, :], 7, None, ALU.logical_shift_right))
            dve.tensor_copy(pos_lo[E, :], lo_i[E, :, :].rearrange("p l c -> p (l c)"))
            link(dve.tensor_copy(pos_hi[E, :], edge_t[E, :, :].rearrange("p l c -> p (l c)")))
            link(dve.tensor_scalar(pad_f[0:1, :, :], pad_base[0:1, :, :], 1.0 / P, None, ALU.mult))
            for l in range(2):
                link(dve.tensor_scalar(bank_f[:, l, :], iota_f[0:1, 0:EDGE_CHUNKS], pad_f[0:1, l, 1:2], None,
                                       ALU.is_ge))
                for b in range(2, NT):
                    link(dve.scalar_tensor_tensor(out=bank_f[:, l, :], in0=iota_f[0:1, 0:EDGE_CHUNKS],
                                                  scalar=pad_f[0:1, l, b:b + 1], in1=bank_f[:, l, :],
                                                  op0=ALU.is_ge, op1=ALU.add))
            dve.tensor_scalar(bank_i[:, :, :], bank_f[:, :, :], 512.0, None, ALU.mult).then_inc(s_bank, 1)

            def sort_hots(r, t, first):
                if not first:
                    dve.wait_ge(s_sorted, COLS_PER_REL * r + COLS_PER_TILE * (t + 1) - COLS_PER_REL)
                for u in range(COLS_PER_TILE):
                    s = COLS_PER_TILE * t + u
                    col = bass.ds(COLS_PER_REL * r + s, 1)
                    dve.tensor_scalar(sort_hot[E, s, 0:P], iota_h[E, 0:P], pos_lo[E, col], None, ALU.is_equal)
                    for v, value in enumerate((node_f, code_f)):
                        at = P + v * EDGE_CHUNKS
                        ins = dve.tensor_scalar(sort_hot[E, s, at:at + EDGE_CHUNKS], iota_h[E, 0:EDGE_CHUNKS],
                                                pos_hi[E, col],
                                                value[E, :, :].rearrange("p l c -> p (l c)")[:, col],
                                                ALU.is_equal, ALU.mult)
                    ins.then_inc(s_hot, 1)

            def dest_hots(l, j, slots):
                for n, s in enumerate(slots):
                    dve.tensor_scalar(dest_hot[:, s, :], iota_h[:, 0:P], dest_f[:, l, bass.ds(j + n, 1)], None,
                                      ALU.is_equal).then_inc(s_dhot, 1)

            def relation(r, q, first, second, i=None):
                for t in range(NT):
                    if t < 2:
                        slot = 2 * (1 - q) + t
                        split_lo(slot, slot, 2 * r + 3 + t)
                    dve.wait_ge(s_tr, NT * r + t + 1)
                    if t == 0:
                        dve.wait_ge(s_bias[q], 16 * (1 if i is None else i + 1))
                    if not (first and t < 2):
                        dve.wait_ge(s_rlo, NT * r + t - 1)
                    dve.scalar_tensor_tensor(out=xn[:, t % 2, :], in0=ps[:, 5 + t % 2, :],
                                             scalar=1.0 / (SX * SW), in1=bias_row[:, q, :],
                                             op0=ALU.mult, op1=ALU.add).then_inc(s_row, 1)
                    sort_hots(r, t, first)
                    if second is not None:
                        s0 = COLS_PER_REL * q + COLS_PER_TILE * t
                        if second > 0:
                            dve.wait_ge(s_seg, COLS_PER_REL * r + (COLS_PER_TILE * (t + 1) - RELS * COLS_PER_REL - SEG))
                        dest_hots(0, COLS_PER_REL * r + (COLS_PER_TILE * t - RELS * COLS_PER_REL),
                                  range(s0, s0 + COLS_PER_TILE))
                    dve.wait_ge(s_rhi, NT * r + t + 1)
                    if t == 0 and i is not None and not (isinstance(i, int) and i == 0):
                        dve.wait_ge(s_store[q], 16 * i)
                    dve.scalar_tensor_tensor(out=rows_out[:, q, t, D:2 * D], in0=xn[:, t % 2, :], scalar=SH,
                                             in1=rows_out[:, q, t, 0:D], op0=ALU.mult, op1=ALU.subtract)\
                        .then_inc(s_rlo, 1)

            def decode(l):
                dve.wait_ge(s_sorted, EC * (l + 1))
                node = ps[:, 7, 0:EDGE_CHUNKS]
                code = ps[:, 7, EDGE_CHUNKS:2 * EDGE_CHUNKS]
                link(dve.tensor_copy(code_i[:, :], code))
                dve.tensor_scalar(part_i[:, 0, :], code_i[:, :], 255, None, ALU.bitwise_and)
                link(dve.tensor_scalar(part_i[:, 1, :], code_i[:, :], 8, None, ALU.logical_shift_right))
                dve.tensor_scalar(dest_f[:, l, :], part_i[:, 0, :], -1.0, None, ALU.add)
                link(dve.tensor_scalar(row_rel[:, :], part_i[:, 1, :], float(PADDED), float(l * RELS * PADDED),
                                       ALU.mult, ALU.add))
                link(dve.tensor_tensor(row_f[:, :], node, row_rel[:, :], ALU.add))
                link(dve.tensor_copy(row_idx[:, l, :], row_f[:, :]))
                dve.sem_inc(s_dec, 1)

            relation(0, 0, True, None, 0)
            relation(1, 1, False, None, 0)
            with dve.Fori(1, RELS // 2) as i:
                relation(2 * i, 0, False, None, i)
                relation(2 * i + 1, 1, False, None, i)
            decode(0)
            half = RELS // 2
            relation(RELS, 0, False, 0, half)
            relation(RELS + 1, 1, False, 0, half)
            with dve.Fori(half + 1, RELS) as i:
                relation(2 * i, 0, False, 1, i)
                relation(2 * i + 1, 1, False, 1, i)
            dest_hots(0, EDGE_CHUNKS - 1, [SEG])
            decode(1)

            dve.wait_ge(s_tr, NT * (2 * RELS + 1))
            for j in range(KH):
                split_lo(j, j % RAW, GNN_CHUNKS + j + 1)
            dve.wait_ge(s_rwh, 1)
            dve.scalar_tensor_tensor(out=rw_lo[:, :], in0=rw_raw[:, :], scalar=SW, in1=rw_hi[:, :],
                                     op0=ALU.mult, op1=ALU.subtract).then_inc(s_rwl, 1)
            dve.tensor_scalar(b1_s[:, :], b1[:, :], SX * SW, None, ALU.mult)
            dve.wait_ge(s_self, NT)
            for t in range(NT):
                ins = dve.tensor_tensor(self_sb(t), self_sb(t), b_self_row[:, :], ALU.add)
            link(ins)
            with dve.Fori(0, 4) as i:
                for g in range(0, SEG, 4):
                    dve.wait_ge(s_seg, SEG * i + (EDGE_CHUNKS - SEG + g + 4))
                    dest_hots(1, SEG * i + g, range(g, g + 4))
            dest_hots(1, EDGE_CHUNKS - 1, [SEG])

            dve.wait_ge(s_seg, 2 * EDGE_CHUNKS)
            for t in range(NT):
                ins = dve.scalar_tensor_tensor(out=self_sb(t), in0=ps[:, t, :], scalar=1.0 / SH,
                                               in1=self_sb(t), op0=ALU.mult, op1=ALU.add)
            link(ins)
            for t in range(NT):
                ins = dve.scalar_tensor_tensor(out=x_sb[:, t, :], in0=self_sb(t), scalar=0.0,
                                               in1=x_sb[:, t, :], op0=ALU.max, op1=ALU.add)
            link(ins)
            layer_norm_part(1)

            dve.wait_ge(s_lg, 1)
            for t in range(NT):
                ins = dve.scalar_tensor_tensor(out=logits[:, t, :], in0=ps[:, 7, t * EXPERTS:(t + 1) * EXPERTS],
                                               scalar=1.0 / (SX * SW), in1=rb_row[:, :],
                                               op0=ALU.mult, op1=ALU.add)
            link(ins)
            for t in range(NT):
                ins = dve.max(top[:, t, :], logits[:, t, :])
            link(ins)
            for t in range(NT):
                ins = dve.max_index(top_i[:, t, :], top[:, t, :], logits[:, t, :])
            dve.tensor_tensor(soft[:, 0, :], top[:, :, 1], top[:, :, 0], ALU.subtract).then_inc(s_dif, 1)
            link(ins) if False else None
            dve.wait_ge(s_exp, 1)
            link(dve.tensor_copy(top_if[:, :, :], top_i[:, :, :]))
            link(dve.tensor_scalar(soft[:, 0, :], soft[:, 1, :], 1.0, None, ALU.add))
            link(dve.reciprocal(soft[:, 2, :], soft[:, 0, :]))
            link(dve.tensor_tensor(soft[:, 3, :], soft[:, 1, :], soft[:, 2, :], ALU.mult))
            for e in range(EXPERTS):
                dve.scalar_tensor_tensor(out=cw_a[:, e, :], in0=top_if[:, :, 0], scalar=float(e),
                                         in1=soft[:, 2, :], op0=ALU.is_equal, op1=ALU.mult)
                ins = dve.scalar_tensor_tensor(out=cw_b[:, e, :], in0=top_if[:, :, 1], scalar=float(e),
                                               in1=soft[:, 3, :], op0=ALU.is_equal, op1=ALU.mult)
            link(ins)
            link(dve.tensor_tensor(cw[:, :, :].rearrange("p t e -> p e t"), cw_a[:, :, :], cw_b[:, :, :], ALU.add))
            dve.tensor_scalar(cw_s[:, :].rearrange("p (e t) -> p e t", t=NT),
                              cw[:, :, :].rearrange("p t e -> p e t"), 1.0 / (SA * SW), None, ALU.mult)\
                .then_inc(s_cw, 1)
            dve.memset(aT_hi[:, :, 2 * TOK:PADDED], 0.0).then_inc(s_free1, 1)
            dve.memset(aT_lo[:, :, 2 * TOK:PADDED], 0.0).then_inc(s_free1, 1)
            dve.wait_ge(s_cwt, 2)
            dve.tensor_copy(cwT[:, 0:4 * P], ps[0:EXPERTS, 6, :])
            dve.tensor_copy(cwT[:, 4 * P:], ps[0:EXPERTS, 7, 128:256]).then_inc(s_cwc, 1)
            for t in range(NT):
                dve.wait_ge(s_b2, t + 1)
                dve.tensor_tensor(acc[:, t, :], ps[:, 4 + t % 4, :], x_sb[:, t, :], ALU.add).then_inc(s_comb, 1)

            def expert(e, last):
                for j in range(KH):
                    for c in range(2):
                        dve.wait_ge(s_silu, 16 * e + 2 * j + c + 1)
                        dve.scalar_tensor_tensor(out=glu[:, c, 0:TOK], in0=ps[:, 2 * c + 1, 0:TOK],
                                                 scalar=b1_s[:, bass.ds(2 * KH * e + KH + j, 1)],
                                                 in1=silu[:, c, 0:TOK], op0=ALU.add, op1=ALU.mult)\
                            .then_inc(s_free1, 1)
                        dve.wait_ge(s_ahi, 16 * e + 2 * j + c + 1)
                        dve.scalar_tensor_tensor(out=aT_lo[:, j, c * TOK:(c + 1) * TOK], in0=glu[:, c, 0:TOK],
                                                 scalar=SA / (SX * SW), in1=aT_hi[:, j, c * TOK:(c + 1) * TOK],
                                                 op0=ALU.mult, op1=ALU.subtract).then_inc(s_alo, 1)
                    if j < 4:
                        n = KH + (j if last else 2 * j)
                        split_lo(KH + j, n % RAW, GNN_CHUNKS + SLOTS * e + n + 1)
                    if not last:
                        n = KH + fc1_order(j)
                        split_lo(j, n % RAW, GNN_CHUNKS + SLOTS * e + n + 1)
                for t in range(NT):
                    dve.wait_ge(s_fc2, NT * e + t + 1)
                    dve.scalar_tensor_tensor(out=acc[:, t, :], in0=ps[:, 4 + t % 4, :],
                                             scalar=cw_s[:, bass.ds(NT * e + t, 1)], in1=acc[:, t, :],
                                             op0=ALU.mult, op1=ALU.add).then_inc(s_comb, 1)

            with dve.Fori(0, EXPERTS - 1) as e:
                expert(e, False)
            last_expert(expert)

        @block.tensor
        def _(pe):
            def product(to, lhs, rhs, terms, skip=False):
                n = 0
                for k in terms:
                    (lh, ll), (rh, rl) = lhs(k), rhs(k)
                    for a, b in ((lh, rh), (lh, rl), (ll, rh)):
                        ins = pe.matmul(to, a, b, start=(n == 0), stop=(n == 3 * len(terms) - 1))
                        n += 1
                return ins

            def layer_norm_part(n):
                for t in range(NT):
                    pe.wait_ge(s_xn, NT * n + t + 1)
                    if t >= 2:
                        pe.wait_ge(s_xlo, NT * n + t - 1)
                    for k in range(KD):
                        ins = pe.transpose(ps[:, 5 + t % 2, k * P:(k + 1) * P], xn[:, t % 2, k * P:(k + 1) * P],
                                           ident[:, :])
                    ins.then_inc(s_xT, 1)

            pe.wait_ge(s_const, 5)
            layer_norm_part(0)
            pe.wait_ge(s_sum, 1)
            pe.matmul(ps[:, 7, 0:2 * NT], before[0:EP, :], part_sum[0:EP, :, :].rearrange("p l b -> p (l b)"),
                      start=True, stop=True)
            pe.matmul(ps[:, 7, 16:16 + 2 * NT], ones[0:EP, 0:P], part_sum[0:EP, :, :].rearrange("p l b -> p (l b)"),
                      start=True, stop=True).then_inc(s_pre, 1)
            pe.wait_ge(s_bank, 1)

            def sum_chunk(slot, hot, bank, n_gathered, n_hot):
                pe.wait_ge(s_gat[slot], n_gathered)
                pe.wait_ge(s_dhot, n_hot)
                for part_at in range(2):
                    ins = pe.matmul(ps_flat[:, bass.ds(bank, D)], dest_hot[:, hot, :],
                                    gathered[:, slot, part_at * D:(part_at + 1) * D], start=False, stop=True,
                                    skip_group_check=True)
                ins.then_inc(s_seg, 1)

            def bank_of(l, j):
                return pe.value_load(bank_i[0:1, l, bass.ds(j, 1)], min_val=0, max_val=(NT - 1) * 512)

            def relation(r, q, first, fresh, second, i=None):
                for t in range(NT):
                    if t == 0:
                        pe.wait_ge(s_wlo, 2 * r + 2)
                    if first and t < 2:
                        pe.wait_ge(s_xlo, NT)
                    else:
                        pe.wait_ge(s_row, NT * r + t - 1)
                    w = lambda k: 2 * q + k // 2
                    product(ps[:, 5 + t % 2, :],
                            lambda k: (xT_hi[:, k, t * P:(t + 1) * P], xT_lo[:, k, t * P:(t + 1) * P]),
                            lambda k: (w_hi[:, w(k), (k % 2) * D:(k % 2 + 1) * D],
                                       w_lo[:, w(k), (k % 2) * D:(k % 2 + 1) * D]),
                            range(KD)).then_inc(s_tr, 1)
                    for u in range(COLS_PER_TILE):
                        s = COLS_PER_TILE * t + u
                        pe.wait_ge(s_hot, COLS_PER_REL * r + s + 1)
                        pe.matmul(ps[:, 7, 0:2 * EDGE_CHUNKS], sort_hot[0:EP, s, 0:P],
                                  sort_hot[0:EP, s, P:P + 2 * EDGE_CHUNKS],
                                  start=(fresh and s == 0), stop=True, skip_group_check=True).then_inc(s_sorted, 1)
                    if second:
                        first_chunk = COLS_PER_REL * r + (COLS_PER_TILE * t - RELS * COLS_PER_REL)
                        s0 = COLS_PER_REL * q + COLS_PER_TILE * t
                        for u in range(COLS_PER_TILE):
                            bank = bank_of(0, first_chunk + u)
                            sum_chunk((s0 + u) % RING, s0 + u, bank,
                                      32 * i + 16 * (q - RELS + 1), first_chunk + u + 1)

            relation(0, 0, True, True, False)
            relation(1, 1, False, False, False)
            with pe.Fori(1, RELS // 2) as i:
                relation(2 * i, 0, False, False, False)
                relation(2 * i + 1, 1, False, False, False)
            pe.wait_ge(s_dec, 1)
            for t in range(NT):
                ins = pe.matmul(ps[:, t, :], zeros[:, 0:P], zeros[:, :], start=True, stop=True)
            half = RELS // 2
            relation(RELS, 0, False, True, True, half)
            relation(RELS + 1, 1, False, False, True, half)
            with pe.Fori(half + 1, RELS) as i:
                relation(2 * i, 0, False, False, True, i)
                relation(2 * i + 1, 1, False, False, True, i)
            sum_chunk(RING, SEG, bank_of(0, EDGE_CHUNKS - 1), 16, EDGE_CHUNKS)
            pe.wait_ge(s_wlo, GNN_CHUNKS)
            for t in range(NT):
                if t < 2:
                    pe.wait_ge(s_row, 2 * RELS * NT)
                else:
                    pe.wait_ge(s_self, t - 1)
                product(ps[:, 5 + t % 2, :],
                        lambda k: (xT_hi[:, k, t * P:(t + 1) * P], xT_lo[:, k, t * P:(t + 1) * P]),
                        lambda k: (w_hi[:, k // 2, (k % 2) * D:(k % 2 + 1) * D],
                                   w_lo[:, k // 2, (k % 2) * D:(k % 2 + 1) * D]),
                        range(KD)).then_inc(s_tr, 1)
            turns = EDGE_CHUNKS // RING
            with pe.Fori(0, 4) as i:
                for s in range(SEG):
                    sum_chunk(s % RING, s, bank_of(1, SEG * i + s), 32 * i + 16 * (turns + s // RING + 1),
                              SEG * i + (EDGE_CHUNKS + s + 1))
            sum_chunk(RING, SEG, bank_of(1, EDGE_CHUNKS - 1), 32, 2 * EDGE_CHUNKS)

            pe.wait_ge(s_self, NT)
            layer_norm_part(1)
            pe.wait_ge(s_xlo, 2 * NT)
            pe.wait_ge(s_rwl, 1)
            pe.wait_ge(s_dec, 2)
            for t in range(NT):
                ins = product(ps[:, 7, t * EXPERTS:(t + 1) * EXPERTS],
                              lambda k: (xT_hi[:, k, t * P:(t + 1) * P], xT_lo[:, k, t * P:(t + 1) * P]),
                              lambda k: (rw_hi[:, k * EXPERTS:(k + 1) * EXPERTS],
                                         rw_lo[:, k * EXPERTS:(k + 1) * EXPERTS]),
                              range(KD))
            ins.then_inc(s_lg, 1)
            pe.wait_ge(s_cw, 1)
            for t in range(NT):
                to = ps[0:EXPERTS, 6, t * P:(t + 1) * P] if t < 4 else ps[0:EXPERTS, 7, 128:256]
                ins = pe.transpose(to, cw[:, t, :], ident[:, :])
                if t >= 3:
                    ins.then_inc(s_cwt, 1)
            pe.wait_ge(s_cwc, 1)
            for t in range(NT):
                if t == 4:
                    pe.wait_ge(s_comb, 1)
                pe.matmul(ps[:, 4 + t % 4, :], cwT[:, t * P:(t + 1) * P], b2[:, :], start=True, stop=True)\
                    .then_inc(s_b2, 1)
            pe.wait_ge(s_wlo, GNN_CHUNKS + KH)

            def expert(e, last):
                for j in range(KH):
                    n = fc1_order(j) - (SLOTS - KH)
                    pe.wait_ge(s_wlo, SLOTS * e + (GNN_CHUNKS + n + 1))
                    for c in range(2):
                        pe.wait_ge(s_free1, 16 * e + 2 * j + c + 1)
                        for half_at in range(2):
                            ins = product(
                                ps[:, 2 * c + half_at, 0:TOK],
                                lambda k: (w_hi[:, j, (2 * k + half_at) * P:(2 * k + half_at + 1) * P],
                                           w_lo[:, j, (2 * k + half_at) * P:(2 * k + half_at + 1) * P]),
                                lambda k: (xT_hi[:, k, c * TOK:(c + 1) * TOK], xT_lo[:, k, c * TOK:(c + 1) * TOK]),
                                range(KD))
                        ins.then_inc(s_fc1, 1)
                for t in range(NT):
                    pe.wait_ge(s_comb, NT * e + (5, 2, 3, 4, 6)[t])
                    m = 0
                    for k in range(KH):
                        if t == 0:
                            pe.wait_ge(s_alo, 16 * e + 2 * k + 2)
                            if k % 2 == 0:
                                pe.wait_ge(s_wlo, SLOTS * e + (GNN_CHUNKS + KH + (k // 2 if last else k) + 1))
                        a_h, a_l = (a[:, k, t * P:(t + 1) * P] for a in (aT_hi, aT_lo))
                        b_h, b_l = (b[:, KH + k // 2, (k % 2) * D:(k % 2 + 1) * D] for b in (w_hi, w_lo))
                        for a, b in ((a_h, b_h), (a_h, b_l), (a_l, b_h)):
                            ins = pe.matmul(ps[:, 4 + t % 4, :], a, b, start=(m == 0), stop=(m == 3 * KH - 1))
                            m += 1
                    ins.then_inc(s_fc2, 1)

            with pe.Fori(0, EXPERTS - 1) as e:
                expert(e, False)
            last_expert(expert)


def last_expert(expert):
    expert(EXPERTS - 1, True)


def kernel(x, src, dst, edge_type_8, L0_gnn_W_self, L0_gnn_b_self, L0_gnn_W_rel, L0_gnn_b_rel,
           L0_ffn_router_w, L0_ffn_router_b, L0_ffn_fc1_w, L0_ffn_fc1_b, L0_ffn_fc2_w, L0_ffn_fc2_b):
    import numpy as np
    import concourse.bacc as bacc
    from concourse.bass_utils import run_bass_kernel_spmd

    gnn = np.concatenate([np.asarray(L0_gnn_W_rel), np.asarray(L0_gnn_W_self)[None]])
    gnn = gnn.transpose(0, 2, 1).reshape(2 * RELS + 1, 2, 2, P, D).transpose(0, 1, 3, 2, 4)
    gnn = gnn.reshape(GNN_CHUNKS, P, CH)
    fc1 = np.asarray(L0_ffn_fc1_w).reshape(EXPERTS, 2, KH, P, KD, P).transpose(0, 2, 5, 4, 1, 3)
    fc1 = fc1.reshape(EXPERTS, KH, P, CH)
    fc2 = np.asarray(L0_ffn_fc2_w).transpose(0, 2, 1).reshape(EXPERTS, 4, 2, P, D).transpose(0, 1, 3, 2, 4)
    fc2 = fc2.reshape(EXPERTS, 4, P, CH)
    stream = [fc1[0, j] for j in range(KH)]
    for e in range(EXPERTS):
        for j in range(KH):
            if j < 4:
                stream.append(fc2[e, j])
            if e + 1 < EXPERTS:
                stream.append(fc1[e + 1, j])
    named = {
        "x": x, "src": src, "dst": dst, "rel": edge_type_8, "gnn_w": gnn,
        "b_self": np.asarray(L0_gnn_b_self)[None], "b_rel": L0_gnn_b_rel,
        "router_w": np.asarray(L0_ffn_router_w).reshape(EXPERTS, KD, P).transpose(2, 1, 0).reshape(P, KD * EXPERTS),
        "router_b": np.asarray(L0_ffn_router_b)[None],
        "ffn_w": np.stack(stream),
        "fc1_b": np.asarray(L0_ffn_fc1_b).reshape(EXPERTS * 2 * KH, P).transpose(1, 0),
        "fc2_b": L0_ffn_fc2_b,
    }
    nc = bacc.Bacc("TRN2", target_bir_lowering=False, num_devices=1)
    arrays, args = {}, []
    for name, a in named.items():
        a = np.ascontiguousarray(a)
        arrays[f"in_{name}"] = a
        args.append(nc.dram_tensor(f"in_{name}", a.shape, mybir.dt.from_np(a.dtype), kind="ExternalInput").ap())
    args.append(nc.dram_tensor("out_x", (NODES, D), F32, kind="ExternalOutput").ap())
    build(nc, *args)
    return run_bass_kernel_spmd(nc, [arrays], core_ids=[0]).results[0]["out_x"]
```

```python
from contextlib import ExitStack

import concourse.bass as bass
from concourse import mybir

F32 = mybir.dt.float32
F16 = mybir.dt.float16
I32 = mybir.dt.int32
U32 = mybir.dt.uint32
ACT = mybir.ActivationFunctionType
ALU = mybir.AluOpType
AX_X = mybir.AxisListType.X

P = 128
NODES = 625
D = 512
KD = D // P
NT = (NODES + P - 1) // P
PADDED = NT * P
LAST = NODES - (NT - 1) * P
EDGES = 20000
RELS = 8
EXPERTS = 8
HID = 1024
KH = HID // P

EP = 125
EC = EDGES // EP
EDGE_CHUNKS = (EDGES + NT * (P - 1)) // P
COLS_PER_REL = EC // RELS
COLS_PER_TILE = COLS_PER_REL // NT
RING = 20
HALF = RING // 2
SEG = 2 * COLS_PER_REL
TAIL = EDGE_CHUNKS - 4 * SEG
assert TAIL == 1 and SEG == 2 * RING

CH = 1024
REL_CHUNKS = 2
GNN_CHUNKS = REL_CHUNKS * (2 * RELS + 1)
SLOTS = 12
COUNTS = 400
RAW = 4
TOK = 313

SX = 64.0
SW = 64.0
SH = 64.0
SA = 16.0
LN_EPS = 1e-5


def fc1_order(j):
    return 2 * j + 1 if j < 4 else 4 + j


def build(nc, x, src, dst, rel, gnn_w, b_self, b_rel, router_w, router_b, ffn_w, fc1_b, fc2_b, out):
    with ExitStack() as ctx:
        def sb(name, shape, dt):
            return ctx.enter_context(nc.sbuf_tensor(name, shape, dt))

        def sem(name):
            return ctx.enter_context(nc.semaphore(name))

        x_sb = sb("x_sb", [P, NT, D], F32)
        xT_hi = sb("xT_hi", [P, KD, PADDED], F16)
        xT_lo = sb("xT_lo", [P, KD, PADDED], F16)
        w_raw = sb("w_raw", [P, RAW, CH], F32)
        w_hi = sb("w_hi", [P, SLOTS, CH], F16)
        w_lo = sb("w_lo", [P, SLOTS, CH], F16)

        def self_sb(t):
            return (w_hi[:, KH + t, :] if t < 4 else w_lo[:, KH, :]).bitcast(F32)

        scratch = sb("scratch", [P, 2 * NT * 1024 + (RING + 1) * 1024 + 20 * 456 + (SEG + 1) * P], F16)
        cut = [0]

        def part(cols):
            cut[0] += cols
            return scratch[:, cut[0] - cols:cut[0]]

        rows_out = part(2 * NT * 1024).rearrange("p (q t c) -> p q t c", q=2, t=NT)
        gathered = part((RING + 1) * 1024).rearrange("p (s c) -> p s c", c=1024)
        sort_hot = part(20 * 456).rearrange("p (s c) -> p s c", c=456)
        countT = sort_hot[:, 0:3, :].rearrange("p s c -> p (s c)")[0:2 * RELS, 0:2 * PADDED].bitcast(F32)
        dest_hot = part((SEG + 1) * P).rearrange("p (s c) -> p s c", c=P)
        cut[0] = 2 * NT * 1024

        def edge_part(rows, dt):
            return part(2 * rows * EC).bitcast(dt).rearrange("p (n c) -> p n c", c=EC)

        edge_in = edge_part(3, I32)
        edge_t = edge_part(2, I32)
        edge_l = edge_part(2, I32)
        tile_f = edge_part(2, F32)
        place = edge_part(2, F32)
        place_i = edge_part(2, I32)
        lo_i = edge_part(2, I32)
        rel_f = edge_part(1, F32)[:, 0, :]
        in_bucket = edge_part(2 * NT, F32).rearrange("p (l b) c -> p l b c", l=2)
        running = edge_part(2 * NT, F32).rearrange("p (l b) c -> p l b c", l=2)
        assert cut[0] <= 2 * NT * 1024 + (RING + 1) * 1024
        cut[0] = 0
        aT_hi = part(KH * PADDED).rearrange("p (k n) -> p k n", n=PADDED)
        aT_lo = part(KH * PADDED).rearrange("p (k n) -> p k n", n=PADDED)
        acc = part(2 * NT * D).bitcast(F32).rearrange("p (t n) -> p t n", t=NT)
        silu = part(2 * 2 * 320).bitcast(F32).rearrange("p (c n) -> p c n", c=2)
        glu = part(2 * 2 * 320).bitcast(F32).rearrange("p (c n) -> p c n", c=2)
        cwT = part(2 * PADDED).bitcast(F32)[0:EXPERTS, :]

        xn = sb("xn", [P, 2, D], F32)
        b_rel_sb = sb("b_rel_sb", [2 * RELS, D], F32)
        rel_hot = sb("rel_hot", [P, 2, EDGE_CHUNKS, RELS], F16)
        count = sb("count", [P, NT, 2 * RELS], F32)
        b_self_row = w_lo[:, KH + 1, :].bitcast(F32)
        ident = sb("ident", [P, P], F32)
        zeros = sb("zeros", [P, D], F16)
        iota_f = sb("iota_f", [P, 176], F32)
        iota_h = sb("iota_h", [P, 176], F16)
        iota_i = sb("iota_i", [P, 176], I32)
        before = sb("before", [P, P], F32)
        ones = sb("ones", [P, EC], F32)
        stats = sb("stats", [P, NT, 6], F32)
        mv = sb("mv", [P, NT, 2], F32)
        rstd = sb("rstd", [P, NT], F32)
        std = sb("std", [P, NT], F32)
        packed = sb("packed", [P, 2, EC, 2], F16)
        packed_pair = packed[:, :, :, :].rearrange("p l c v -> p (l c v)").bitcast(F32)
        part_sum = sb("part_sum", [P, 2, NT], F32)
        pad_i = sb("pad_i", [P, 2, NT], I32)
        pad_f = sb("pad_f", [P, 2, NT], F32)
        pad_end = sb("pad_end", [P, 2, NT], F32)
        pad_base = sb("pad_base", [P, 2, NT], F32)
        offset = sb("offset", [P, 2, NT], F32)
        pos_lo = sb("pos_lo", [P, 2 * EC], F32)
        pos_hi = sb("pos_hi", [P, 2 * EC], F32)
        bank_f = sb("bank_f", [1, 2, EDGE_CHUNKS], F32)
        bank_i = sb("bank_i", [1, 2, EDGE_CHUNKS + 3], I32)
        code_i = sb("code_i", [P, EDGE_CHUNKS], I32)
        part_i = sb("part_i", [P, 2, EDGE_CHUNKS], I32)
        dest_f = sb("dest_f", [P, 2, EDGE_CHUNKS], F32)
        row_f = sb("row_f", [P, EDGE_CHUNKS], F32)
        row_rel = sb("row_rel", [P, EDGE_CHUNKS], F32)
        row_idx = sb("row_idx", [P, 2, EDGE_CHUNKS], U32)
        ring_idx = sb("ring_idx", [P, RING + 1], U32)
        rw_raw = sb("rw_raw", [P, KD * EXPERTS], F32)
        rw_hi = sb("rw_hi", [P, KD * EXPERTS], F16)
        rw_lo = sb("rw_lo", [P, KD * EXPERTS], F16)
        rb_row = sb("rb_row", [P, EXPERTS], F32)
        logits = sb("logits", [P, NT, EXPERTS], F32)
        top = sb("top", [P, NT, 8], F32)
        top_i = sb("top_i", [P, NT, 8], U32)
        top_if = sb("top_if", [P, NT, 8], F32)
        soft = sb("soft", [P, 4, NT], F32)
        cw_a = sb("cw_a", [P, EXPERTS, NT], F32)
        cw_b = sb("cw_b", [P, EXPERTS, NT], F32)
        cw = sb("cw", [P, NT, EXPERTS], F32)
        cw_s = sb("cw_s", [P, EXPERTS * NT], F32)
        b1 = sb("b1", [P, EXPERTS * 2 * KH], F32)
        b1_s = sb("b1_s", [P, EXPERTS * 2 * KH], F32)
        b2 = sb("b2", [EXPERTS, D], F32)
        ps = ctx.enter_context(nc.psum_tensor("ps", [P, 8, 512], F32))
        ps_flat = ps[:, :, :].rearrange("p b n -> p (b n)")
        rows_dram = nc.dram_tensor("rows_dram", [2 * RELS * PADDED, 2 * D], F16, kind="Internal").ap()
        rows_by_rel = rows_dram.rearrange("(r t p) c -> p r t c", p=P, t=NT)

        s_x = sem("x_loaded")
        s_xpad = sem("x_pad_zeroed")
        s_edges = sem("edges_loaded")
        s_small = sem("small_loaded")
        s_raw = [sem(f"w_raw_loaded{s}") for s in range(RAW)]
        s_const = sem("consts_ready")
        s_pool = sem("pool_chain")
        s_dve = sem("dve_chain")
        s_var = sem("var_ready")
        s_std = sem("std_ready")
        s_xn = sem("xn_ready")
        s_xT = sem("xn_transposed")
        s_xhi = sem("xT_hi_ready")
        s_xlo = sem("xT_lo_ready")
        s_whi = sem("w_hi_ready")
        s_wlo = sem("w_lo_ready")
        s_sum = sem("part_sum_ready")
        s_pre = sem("prefix_done")
        s_bank = sem("bank_table_ready")
        s_hot = sem("sort_hot_ready")
        s_sorted = sem("column_sorted")
        s_dec = sem("list_decoded")
        s_tr = sem("transformed")
        s_brel = sem("b_rel_loaded")
        s_cnt = sem("counts_ready")
        s_cntt = sem("counts_transposed")
        s_cntc = sem("countT_copied")
        s_bsum = sem("biases_summed")
        s_rhi = sem("row_hi_ready")
        s_rlo = sem("row_lo_ready")
        s_store = [sem(f"rows_stored{q}") for q in range(2)]
        s_idx = sem("idx_copied")
        s_gat = [sem(f"gathered{s}") for s in range(RING + 1)]
        s_dhot = sem("dest_hot_ready")
        s_seg = sem("chunk_summed")
        s_zero = sem("sums_zeroed")
        s_self = sem("self_evacuated")
        s_gnn = sem("gnn_out_ready")
        s_lg = sem("logits_ready")
        s_dif = sem("top_diff_ready")
        s_exp = sem("top_exp_ready")
        s_cw = sem("cw_ready")
        s_cwt = sem("cw_transposed")
        s_cwc = sem("cwT_copied")
        s_b2 = sem("bias2_summed")
        s_fc1 = sem("fc1_done")
        s_silu = sem("silu_ready")
        s_turn = sem("silu_turn")
        s_free1 = sem("fc1_pair_free")
        s_ahi = sem("a_hi_ready")
        s_alo = sem("a_lo_ready")
        s_fc2 = sem("fc2_done")
        s_comb = sem("combined")
        s_rwh = sem("router_hi_ready")
        s_rwl = sem("router_lo_ready")
        s_out = sem("out_stored")

        block = ctx.enter_context(nc.Block())

        @block.sync
        def _(sp):
            for n, a in enumerate((src, dst, rel)):
                sp.dma_start(edge_in[0:EP, n, :], a.rearrange("(p c) -> p c", c=EC)).then_inc(s_edges, 16)
            sp.dma_start(x_sb[:, 0:NT - 1, :],
                         x[0:(NT - 1) * P, :].rearrange("(t p) d -> p t d", p=P)).then_inc(s_x, 16)
            sp.wait_ge(s_xpad, 1)
            sp.dma_start(x_sb[0:LAST - 1, NT - 1, :], x[(NT - 1) * P:NODES - 1, :]).then_inc(s_x, 16)
            sp.dma_start(x_sb[LAST - 1:LAST, NT - 1, :], x[NODES - 1:NODES, :]).then_inc(s_x, 16)

            def load_gnn(chunk, slot):
                sp.dma_start(w_raw[:, slot, :], gnn_w[bass.ds(chunk, 1), :, :].rearrange("a p c -> p (a c)"))\
                    .then_inc(s_raw[slot], 16)

            load_gnn(0, 0)
            load_gnn(1, 1)
            sp.dma_start(b_rel_sb[:, :], b_rel).then_inc(s_brel, 16)
            sp.dma_start(b_self_row[:, :], b_self.to_broadcast([P, D])).then_inc(s_small, 16)
            sp.dma_start(rw_raw[:, :], router_w).then_inc(s_small, 16)
            sp.dma_start(rb_row[:, :], router_b.to_broadcast([P, EXPERTS])).then_inc(s_small, 16)
            sp.dma_start(b1[:, :], fc1_b).then_inc(s_small, 16)
            sp.dma_start(b2[:, :], fc2_b).then_inc(s_small, 16)

            def relation(r, q):
                sp.wait_ge(s_wlo, 2 * r + 2)
                load_gnn(2 * r + 2, 2 * (1 - q))
                load_gnn(2 * r + 3, 2 * (1 - q) + 1)
                sp.wait_ge(s_rlo, NT * (r + 1))
                sp.dma_start(rows_by_rel[:, bass.ds(r, 1), :, :].rearrange("p r t c -> p (r t) c"),
                             rows_out[:, q, :, :]).then_inc(s_store[q], 16)

            with sp.Fori(0, RELS) as i:
                relation(2 * i, 0)
                relation(2 * i + 1, 1)

            with sp.Fori(0, EXPERTS * SLOTS // RAW) as i:
                for s in range(RAW):
                    sp.wait_ge(s_wlo, GNN_CHUNKS - RAW + RAW * i + s + 1)
                    sp.dma_start(w_raw[:, s, :],
                                 ffn_w[bass.ds(RAW * i + s, 1), :, :].rearrange("a p c -> p (a c)"))\
                        .then_inc(s_raw[s], 16)
            for t in range(NT):
                sp.wait_ge(s_comb, NT * EXPERTS + t + 1)
                if t < NT - 1:
                    sp.dma_start(out[t * P:(t + 1) * P, :], acc[:, t, :]).then_inc(s_out, 16)
                else:
                    sp.dma_start(out[t * P:NODES - 1, :], acc[0:LAST - 1, t, :]).then_inc(s_out, 16)
                    sp.dma_start(out[NODES - 1:NODES, :], acc[LAST - 1:LAST, t, :]).then_inc(s_out, 16)
            sp.wait_ge(s_store[0], 16 * RELS)
            sp.wait_ge(s_store[1], 16 * RELS)
            sp.wait_ge(s_out, 16 * (NT + 1))

        @block.gpsimd
        def _(pool):
            links = [0]

            def link(ins):
                links[0] += 1
                ins.then_inc(s_pool, 1)
                pool.wait_ge(s_pool, links[0])

            link(pool.memset(ident[:, :], 0.0))
            pool.affine_select(out=ident[:, :], in_=ident[:, :], compare_op=ALU.not_equal, fill=1.0, base=0,
                               pattern=[[-1, P]], channel_multiplier=1).then_inc(s_const, 1)
            link(pool.memset(before[:, :], 0.0))
            pool.affine_select(out=before[:, :], in_=before[:, :], compare_op=ALU.is_ge, fill=1.0, base=0,
                               pattern=[[-1, P]], channel_multiplier=1).then_inc(s_const, 1)
            link(pool.iota(iota_i[:, :], pattern=[[1, 176]], base=0, channel_multiplier=0))
            link(pool.tensor_copy(iota_f[:, :], iota_i[:, :]))
            pool.tensor_copy(iota_h[:, :], iota_f[:, :]).then_inc(s_const, 1)
            pool.memset(zeros[:, :], 0.0).then_inc(s_const, 1)
            pool.memset(ones[:, :], 1.0).then_inc(s_const, 1)

            def gather(l, slot):
                pool.indirect_dma_start(gathered[:, slot, :], None, rows_dram[0:(l + 1) * RELS * PADDED, :],
                                        bass.IndirectOffsetOnAxis(ap=ring_idx[:, slot:slot + 1], axis=0))\
                    .then_inc(s_gat[slot], 16)

            def gather_half(l, a, h, batch, summed):
                if summed is not None:
                    pool.wait_ge(s_seg, summed)
                    pool.sem_inc(s_idx, 1)
                at = l * EDGE_CHUNKS + RING * a + HALF * h
                pool.tensor_copy(ring_idx[:, HALF * h:HALF * h + HALF],
                                 row_idx[:, :, :].rearrange("p l c -> p (l c)")[:, bass.ds(at, HALF)])\
                    .then_inc(s_idx, 1)
                pool.wait_ge(s_idx, batch)
                pool.sem_inc(s_pool, 1)
                for s in range(HALF * h, HALF * h + HALF):
                    gather(l, s)

            turns = EDGE_CHUNKS // RING
            for l in range(2):
                pool.wait_ge(s_dec, l + 1)
                for q in range(2):
                    pool.wait_ge(s_store[q], 16 * (RELS // 2) * (l + 1))
                base = l * (4 * turns - 2 + 1)
                for h in range(2):
                    gather_half(l, 0, h, base + (h + 1) * (1 + l), None if l == 0 else
                                EDGE_CHUNKS - TAIL - RING + HALF * (h + 1))
                first = base + 2 * (1 + l)
                with pool.Fori(1, turns) as a:
                    for h in range(2):
                        gather_half(l, a, h, 4 * a + (first - 4 + 2 * (h + 1)),
                                    RING * a + (l * EDGE_CHUNKS - RING + HALF * (h + 1)))
                if l == 1:
                    pool.wait_ge(s_seg, EDGE_CHUNKS)
                pool.tensor_copy(ring_idx[:, RING:RING + 1],
                                 row_idx[:, l, EDGE_CHUNKS - 1:EDGE_CHUNKS]).then_inc(s_idx, 1)
                pool.wait_ge(s_idx, first + 4 * (turns - 1) + 1)
                gather(l, RING)

        @block.scalar
        def _(act):
            def split_hi(slot, raw, loaded):
                act.wait_ge(s_raw[raw], loaded)
                act.activation(w_hi[:, slot, :], w_raw[:, raw, :], ACT.Copy, scale=SW).then_inc(s_whi, 1)

            def layer_norm_part(n):
                act.wait_ge(s_var, n + 1)
                act.activation(std[:, :], rstd[:, :], ACT.Sqrt).then_inc(s_std, 1)
                for t in range(NT):
                    act.wait_ge(s_xT, NT * n + t + 1)
                    act.activation(xT_hi[:, :, t * P:(t + 1) * P],
                                   ps[:, 5 + t % 2, :].rearrange("p (k m) -> p k m", k=KD),
                                   ACT.Copy, scale=SX).then_inc(s_xhi, 1)

            layer_norm_part(0)
            split_hi(0, 0, 16)
            split_hi(1, 1, 16)
            act.wait_ge(s_small, 16 * 5)
            act.activation(rw_hi[:, :], rw_raw[:, :], ACT.Copy, scale=SW).then_inc(s_rwh, 1)

            def relation(r, q, i):
                for t in range(NT):
                    if t >= NT - 2:
                        slot = 2 * (1 - q) + t - (NT - 2)
                        if t == NT - 2 and not (isinstance(r, int) and r == 0):
                            act.wait_ge(s_tr, NT * r)
                        split_hi(slot, slot, 16 * (i + 1) + 16 * q)
                    act.wait_ge(s_tr, NT * r + t + 1)
                    if t == 0 and not (isinstance(i, int) and i == 0):
                        act.wait_ge(s_store[q], 16 * i)
                    act.activation(rows_out[:, q, t, 0:D], ps[:, 5 + (q + t) % 2, :], ACT.Copy,
                                   scale=SH / (SX * SW)).then_inc(s_rhi, 1)

            relation(0, 0, 0)
            relation(1, 1, 0)
            with act.Fori(1, RELS) as i:
                relation(2 * i, 0, i)
                relation(2 * i + 1, 1, i)
            for t in range(NT):
                act.wait_ge(s_tr, 2 * RELS * NT + t + 1)
                act.activation(self_sb(t), ps[:, 5 + t % 2, :], ACT.Copy, scale=1.0 / (SX * SW))\
                    .then_inc(s_self, 1)

            def split_ffn(slot, n):
                raw = n[1]
                used = GNN_CHUNKS // RAW + (1 if raw < GNN_CHUNKS % RAW else 0)
                split_hi(slot, raw, 16 * (n[0] + used + 1))

            for j in range(KH):
                split_ffn(j, (j // RAW, j % RAW))
            layer_norm_part(1)
            act.wait_ge(s_dif, 1)
            act.activation(soft[:, 1, :], soft[:, 0, :], ACT.Exp).then_inc(s_exp, 1)

            def expert(e, last):
                for j in range(KH):
                    for c in range(2):
                        act.wait_ge(s_fc1, 16 * e + 2 * j + c + 1)
                        act.sem_inc(s_turn, 1)
                        act.activation(silu[:, c, 0:TOK], ps[:, 2 * c, 0:TOK], ACT.Silu,
                                       bias=b1[:, bass.ds(2 * KH * e + j, 1)], scale=1.0 / (SX * SW))\
                            .then_inc(s_silu, 1)
                        act.wait_ge(s_free1, 16 * e + 2 * j + c + 3)
                        act.activation(aT_hi[:, j, c * TOK:(c + 1) * TOK], glu[:, c, 0:TOK], ACT.Copy,
                                       scale=SA / (SX * SW)).then_inc(s_ahi, 1)
                    if j < 4:
                        n = KH + (j if last else 2 * j)
                        split_ffn(KH + j, (3 * e + n // RAW, n % RAW))
                    if not last:
                        n = KH + fc1_order(j)
                        split_ffn(j, (3 * e + n // RAW, n % RAW))

            with act.Fori(0, EXPERTS - 1) as e:
                expert(e, False)
            last_expert(expert)

        @block.vector
        def _(dve):
            links = [0]

            def link(ins):
                links[0] += 1
                ins.then_inc(s_dve, 1)
                dve.wait_ge(s_dve, links[0])

            def split_lo(slot, raw, hi_count):
                dve.wait_ge(s_whi, hi_count)
                dve.scalar_tensor_tensor(out=w_lo[:, slot, :], in0=w_raw[:, raw, :], scalar=SW,
                                         in1=w_hi[:, slot, :], op0=ALU.mult, op1=ALU.subtract)\
                    .then_inc(s_wlo, 1)

            def layer_norm_part(n):
                for t in range(NT):
                    if n == 0:
                        if t == 0:
                            dve.wait_ge(s_x, 48)
                    ins = dve.bn_stats(stats[:, t, :], x_sb[:, t, :])
                link(ins)
                for t in range(NT):
                    ins = dve.bn_aggr(mv[:, t, :], stats[:, t, :])
                link(ins)
                dve.tensor_scalar(rstd[:, :], mv[:, :, 1], LN_EPS, None, ALU.add).then_inc(s_var, 1)
                dve.wait_ge(s_std, n + 1)
                link(dve.reciprocal(rstd[:, :], std[:, :]))

                def normalise(t):
                    if t >= 2:
                        dve.wait_ge(s_xT, NT * n + t - 1)
                    dve.tensor_scalar(xn[:, t % 2, :], x_sb[:, t, :], mv[:, t, 0:1], rstd[:, t:t + 1],
                                      ALU.subtract, ALU.mult).then_inc(s_xn, 1)

                def low(t):
                    dve.wait_ge(s_xhi, NT * n + t + 1)
                    dve.scalar_tensor_tensor(
                        out=xT_lo[:, :, t * P:(t + 1) * P],
                        in0=ps[:, 5 + t % 2, :].rearrange("p (k m) -> p k m", k=KD), scalar=SX,
                        in1=xT_hi[:, :, t * P:(t + 1) * P], op0=ALU.mult, op1=ALU.subtract)\
                        .then_inc(s_xlo, 1)

                for t in range(NT):
                    normalise(t)
                    if t >= 1:
                        low(t - 1)
                low(NT - 1)

            dve.memset(x_sb[96:P, NT - 1, :], 0.0).then_inc(s_xpad, 1)
            layer_norm_part(0)
            split_lo(0, 0, 1)
            split_lo(1, 1, 2)

            E = slice(0, EP)
            dve.wait_ge(s_edges, 48)
            dve.wait_ge(s_const, 5)
            dve.tensor_scalar(edge_t[E, :, :], edge_in[E, 0:2, :], 7, None, ALU.logical_shift_right)
            link(dve.tensor_scalar(edge_l[E, :, :], edge_in[E, 0:2, :], P - 1, None, ALU.bitwise_and))
            dve.tensor_copy(tile_f[E, :, :], edge_t[E, :, :])
            dve.tensor_copy(place[E, :, :], edge_l[E, :, :])
            dve.tensor_copy(packed[E, 0, :, 0], edge_in[E, 1, :])
            dve.tensor_copy(packed[E, 1, :, 0], edge_in[E, 0, :])
            link(dve.tensor_copy(rel_f[E, :], edge_in[E, 2, :]))
            link(dve.tensor_scalar(rel_f[E, :], rel_f[E, :], 256.0, 1.0, ALU.mult, ALU.add))
            for l in range(2):
                dve.tensor_tensor(packed[E, l, :, 1], place[E, l, :], rel_f[E, :], ALU.add)
            for l in range(2):
                for b in range(NT):
                    ins = dve.tensor_scalar(in_bucket[E, l, b, :], tile_f[E, l, :], float(b), None, ALU.is_equal)
            link(ins)
            for l in range(2):
                for b in range(NT):
                    ins = dve.tensor_tensor_scan(running[E, l, b, :], ones[E, :], in_bucket[E, l, b, :], 0.0,
                                                 ALU.mult, ALU.add)
            link(ins)
            dve.tensor_copy(part_sum[E, :, :], running[E, :, :, EC - 1]).then_inc(s_sum, 1)
            dve.wait_ge(s_pre, 1)
            early = ps[:, 7, 0:2 * NT].rearrange("p (l b) -> p l b", l=2)
            total = ps[:, 7, 16:16 + 2 * NT].rearrange("p (l b) -> p l b", l=2)
            link(dve.tensor_scalar(pad_f[:, :, :], total, float(P - 1), None, ALU.add))
            link(dve.tensor_copy(pad_i[:, :, :], pad_f[:, :, :]))
            link(dve.tensor_scalar(pad_i[:, :, :], pad_i[:, :, :], -P, None, ALU.bitwise_and))
            link(dve.tensor_copy(pad_f[:, :, :], pad_i[:, :, :]))
            for l in range(2):
                ins = dve.tensor_tensor_scan(pad_end[:, l, :], ones[:, 0:NT], pad_f[:, l, :], 0.0, ALU.mult, ALU.add)
            link(ins)
            link(dve.tensor_tensor(pad_base[:, :, :], pad_end[:, :, :], pad_f[:, :, :], ALU.subtract))
            link(dve.scalar_tensor_tensor(out=offset[E, :, :], in0=pad_base[E, :, :], scalar=-1.0,
                                          in1=early[E, :, :], op0=ALU.add, op1=ALU.add))
            for l in range(2):
                for b in range(NT):
                    ins = dve.scalar_tensor_tensor(out=running[E, l, b, :], in0=running[E, l, b, :],
                                                   scalar=offset[E, l, b:b + 1], in1=in_bucket[E, l, b, :],
                                                   op0=ALU.add, op1=ALU.mult)
            link(ins)
            link(dve.tensor_tensor(place[E, :, :], running[E, :, 0, :], running[E, :, 1, :], ALU.add))
            for b in range(2, NT):
                link(dve.tensor_tensor(place[E, :, :], place[E, :, :], running[E, :, b, :], ALU.add))
            link(dve.tensor_copy(place_i[E, :, :], place[E, :, :]))
            dve.tensor_scalar(lo_i[E, :, :], place_i[E, :, :], P - 1, None, ALU.bitwise_and)
            link(dve.tensor_scalar(edge_t[E, :, :], place_i[E, :, :], 7, None, ALU.logical_shift_right))
            dve.tensor_copy(pos_lo[E, :], lo_i[E, :, :].rearrange("p l c -> p (l c)"))
            link(dve.tensor_copy(pos_hi[E, :], edge_t[E, :, :].rearrange("p l c -> p (l c)")))
            link(dve.tensor_scalar(pad_f[0:1, :, :], pad_base[0:1, :, :], 1.0 / P, None, ALU.mult))
            for l in range(2):
                link(dve.tensor_scalar(bank_f[:, l, :], iota_f[0:1, 0:EDGE_CHUNKS], pad_f[0:1, l, 1:2], None,
                                       ALU.is_ge))
                for b in range(2, NT):
                    link(dve.scalar_tensor_tensor(out=bank_f[:, l, :], in0=iota_f[0:1, 0:EDGE_CHUNKS],
                                                  scalar=pad_f[0:1, l, b:b + 1], in1=bank_f[:, l, :],
                                                  op0=ALU.is_ge, op1=ALU.add))
            dve.tensor_copy(bank_i[:, :, 0:EDGE_CHUNKS], bank_f[:, :, :]).then_inc(s_bank, 1)

            def sort_hots(r, t, first):
                if not first:
                    dve.wait_ge(s_sorted, COLS_PER_REL * r + COLS_PER_TILE * (t + 1) - COLS_PER_REL)
                for u in range(COLS_PER_TILE):
                    s = COLS_PER_TILE * t + u
                    col = bass.ds(COLS_PER_REL * r + s, 1)
                    dve.tensor_scalar(sort_hot[E, s, 0:P], iota_h[E, 0:P], pos_lo[E, col], None, ALU.is_equal)
                    dve.tensor_scalar(sort_hot[E, s, P:P + 2 * EDGE_CHUNKS].bitcast(F32), iota_f[E, 0:EDGE_CHUNKS],
                                      pos_hi[E, col], packed_pair[E, col], ALU.is_equal, ALU.mult)\
                        .then_inc(s_hot, 1)

            def dest_hots(l, j, slots):
                for n, s in enumerate(slots):
                    dve.tensor_scalar(dest_hot[:, s, :], iota_h[:, 0:P], dest_f[:, l, bass.ds(j + n, 1)], None,
                                      ALU.is_equal).then_inc(s_dhot, 1)

            def relation(r, q, first, second):
                for t in range(NT):
                    if t >= NT - 2:
                        slot = 2 * (1 - q) + t - (NT - 2)
                        split_lo(slot, slot, 2 * r + 3 + t - (NT - 2))
                    sort_hots(r, t, first)
                    if second is not None:
                        s0 = COLS_PER_REL * q + COLS_PER_TILE * t
                        if second > 0:
                            dve.wait_ge(s_seg, COLS_PER_REL * r + (COLS_PER_TILE * (t + 1) - RELS * COLS_PER_REL - SEG))
                        dest_hots(0, COLS_PER_REL * r + (COLS_PER_TILE * t - RELS * COLS_PER_REL),
                                  range(s0, s0 + COLS_PER_TILE))
                    dve.wait_ge(s_rhi, NT * r + t + 1)
                    dve.scalar_tensor_tensor(out=rows_out[:, q, t, D:2 * D], in0=ps[:, 5 + (q + t) % 2, :],
                                             scalar=SH / (SX * SW), in1=rows_out[:, q, t, 0:D],
                                             op0=ALU.mult, op1=ALU.subtract).then_inc(s_rlo, 1)

            def decode(l):
                dve.wait_ge(s_sorted, EC * (l + 1))
                node = ps[:, 7, 0:2 * EDGE_CHUNKS:2]
                code = ps[:, 7, 1:2 * EDGE_CHUNKS:2]
                link(dve.tensor_copy(code_i[:, :], code))
                dve.tensor_scalar(part_i[:, 0, :], code_i[:, :], 255, None, ALU.bitwise_and)
                link(dve.tensor_scalar(part_i[:, 1, :], code_i[:, :], 8, None, ALU.logical_shift_right))
                dve.tensor_scalar(dest_f[:, l, :], part_i[:, 0, :], -1.0, None, ALU.add)
                link(dve.tensor_scalar(row_rel[:, :], part_i[:, 1, :], float(PADDED), float(l * RELS * PADDED),
                                       ALU.mult, ALU.add))
                link(dve.tensor_tensor(row_f[:, :], node, row_rel[:, :], ALU.add))
                for v in range(RELS):
                    dve.tensor_scalar(rel_hot[:, l, :, v], part_i[:, 1, :], float(v), None, ALU.is_equal)
                dve.tensor_copy(row_idx[:, l, :], row_f[:, :]).then_inc(s_dec, 1)

            relation(0, 0, True, None)
            relation(1, 1, False, None)
            with dve.Fori(1, RELS // 2) as i:
                relation(2 * i, 0, False, None)
                relation(2 * i + 1, 1, False, None)
            decode(0)
            half = RELS // 2
            relation(RELS, 0, False, 0)
            relation(RELS + 1, 1, False, 0)
            with dve.Fori(half + 1, RELS) as i:
                relation(2 * i, 0, False, 1)
                relation(2 * i + 1, 1, False, 1)
            dest_hots(0, EDGE_CHUNKS - 1, [SEG])
            dve.wait_ge(s_seg, EDGE_CHUNKS)
            decode(1)

            dve.wait_ge(s_tr, NT * (2 * RELS + 1))
            for j in range(KH):
                split_lo(j, j % RAW, GNN_CHUNKS + j + 1)
            dve.wait_ge(s_rwh, 1)
            dve.scalar_tensor_tensor(out=rw_lo[:, :], in0=rw_raw[:, :], scalar=SW, in1=rw_hi[:, :],
                                     op0=ALU.mult, op1=ALU.subtract).then_inc(s_rwl, 1)
            dve.tensor_scalar(b1_s[:, :], b1[:, :], SX * SW, None, ALU.mult)
            dve.wait_ge(s_self, NT)
            for t in range(NT):
                ins = dve.tensor_tensor(self_sb(t), self_sb(t), b_self_row[:, :], ALU.add)
            link(ins)
            with dve.Fori(0, 4) as i:
                for g in range(0, SEG, 4):
                    dve.wait_ge(s_seg, SEG * i + (EDGE_CHUNKS - SEG + g + 4))
                    dest_hots(1, SEG * i + g, range(g, g + 4))
            dest_hots(1, EDGE_CHUNKS - 1, [SEG])

            dve.wait_ge(s_seg, 2 * EDGE_CHUNKS)
            dve.tensor_scalar(count[:, :, :], ps[:, 7, COUNTS:COUNTS + 2 * RELS * NT].rearrange(
                "p (t r) -> p t r", t=NT), SH, None, ALU.mult).then_inc(s_cnt, 1)
            dve.wait_ge(s_cntt, 1)
            dve.tensor_copy(countT[:, 0:4 * P], ps[0:2 * RELS, 5, :])
            dve.tensor_copy(countT[:, 4 * P:], ps[0:2 * RELS, 6, 0:P]).then_inc(s_cntc, 1)
            dve.wait_ge(s_bsum, 1)
            for t in range(NT):
                ins = dve.scalar_tensor_tensor(out=self_sb(t), in0=ps[:, t, :], scalar=1.0 / SH,
                                               in1=self_sb(t), op0=ALU.mult, op1=ALU.add)
            link(ins)
            for t in range(NT):
                ins = dve.scalar_tensor_tensor(out=x_sb[:, t, :], in0=self_sb(t), scalar=0.0,
                                               in1=x_sb[:, t, :], op0=ALU.max, op1=ALU.add)
            link(ins)
            layer_norm_part(1)

            dve.wait_ge(s_lg, 1)
            for t in range(NT):
                ins = dve.scalar_tensor_tensor(out=logits[:, t, :], in0=ps[:, 7, t * EXPERTS:(t + 1) * EXPERTS],
                                               scalar=1.0 / (SX * SW), in1=rb_row[:, :],
                                               op0=ALU.mult, op1=ALU.add)
            link(ins)
            for t in range(NT):
                ins = dve.max(top[:, t, :], logits[:, t, :])
            link(ins)
            for t in range(NT):
                ins = dve.max_index(top_i[:, t, :], top[:, t, :], logits[:, t, :])
            dve.tensor_tensor(soft[:, 0, :], top[:, :, 1], top[:, :, 0], ALU.subtract).then_inc(s_dif, 1)
            link(ins) if False else None
            dve.wait_ge(s_exp, 1)
            link(dve.tensor_copy(top_if[:, :, :], top_i[:, :, :]))
            link(dve.tensor_scalar(soft[:, 0, :], soft[:, 1, :], 1.0, None, ALU.add))
            link(dve.reciprocal(soft[:, 2, :], soft[:, 0, :]))
            link(dve.tensor_tensor(soft[:, 3, :], soft[:, 1, :], soft[:, 2, :], ALU.mult))
            for e in range(EXPERTS):
                dve.scalar_tensor_tensor(out=cw_a[:, e, :], in0=top_if[:, :, 0], scalar=float(e),
                                         in1=soft[:, 2, :], op0=ALU.is_equal, op1=ALU.mult)
                ins = dve.scalar_tensor_tensor(out=cw_b[:, e, :], in0=top_if[:, :, 1], scalar=float(e),
                                               in1=soft[:, 3, :], op0=ALU.is_equal, op1=ALU.mult)
            link(ins)
            link(dve.tensor_tensor(cw[:, :, :].rearrange("p t e -> p e t"), cw_a[:, :, :], cw_b[:, :, :], ALU.add))
            dve.tensor_scalar(cw_s[:, :].rearrange("p (e t) -> p e t", t=NT),
                              cw[:, :, :].rearrange("p t e -> p e t"), 1.0 / (SA * SW), None, ALU.mult)\
                .then_inc(s_cw, 1)
            dve.memset(aT_hi[:, :, 2 * TOK:PADDED], 0.0).then_inc(s_free1, 1)
            dve.memset(aT_lo[:, :, 2 * TOK:PADDED], 0.0).then_inc(s_free1, 1)
            dve.wait_ge(s_cwt, 2)
            dve.tensor_copy(cwT[:, 0:4 * P], ps[0:EXPERTS, 6, :])
            dve.tensor_copy(cwT[:, 4 * P:], ps[0:EXPERTS, 7, 128:256]).then_inc(s_cwc, 1)
            for t in range(NT):
                dve.wait_ge(s_b2, t + 1)
                dve.tensor_tensor(acc[:, t, :], ps[:, 4 + t % 4, :], x_sb[:, t, :], ALU.add).then_inc(s_comb, 1)

            def expert(e, last):
                for j in range(KH):
                    for c in range(2):
                        dve.wait_ge(s_silu, 16 * e + 2 * j + c + 1)
                        dve.scalar_tensor_tensor(out=glu[:, c, 0:TOK], in0=ps[:, 2 * c + 1, 0:TOK],
                                                 scalar=b1_s[:, bass.ds(2 * KH * e + KH + j, 1)],
                                                 in1=silu[:, c, 0:TOK], op0=ALU.add, op1=ALU.mult)\
                            .then_inc(s_free1, 1)
                        dve.wait_ge(s_ahi, 16 * e + 2 * j + c + 1)
                        dve.scalar_tensor_tensor(out=aT_lo[:, j, c * TOK:(c + 1) * TOK], in0=glu[:, c, 0:TOK],
                                                 scalar=SA / (SX * SW), in1=aT_hi[:, j, c * TOK:(c + 1) * TOK],
                                                 op0=ALU.mult, op1=ALU.subtract).then_inc(s_alo, 1)
                    if j < 4:
                        n = KH + (j if last else 2 * j)
                        split_lo(KH + j, n % RAW, GNN_CHUNKS + SLOTS * e + n + 1)
                    if not last:
                        n = KH + fc1_order(j)
                        split_lo(j, n % RAW, GNN_CHUNKS + SLOTS * e + n + 1)
                for t in range(NT):
                    dve.wait_ge(s_fc2, NT * e + t + 1)
                    dve.scalar_tensor_tensor(out=acc[:, t, :], in0=ps[:, 4 + t % 4, :],
                                             scalar=cw_s[:, bass.ds(NT * e + t, 1)], in1=acc[:, t, :],
                                             op0=ALU.mult, op1=ALU.add).then_inc(s_comb, 1)

            with dve.Fori(0, EXPERTS - 1) as e:
                expert(e, False)
            last_expert(expert)

        @block.tensor
        def _(pe):
            def product(to, lhs, rhs, terms, skip=False):
                n = 0
                for k in terms:
                    (lh, ll), (rh, rl) = lhs(k), rhs(k)
                    for a, b in ((lh, rh), (lh, rl), (ll, rh)):
                        ins = pe.matmul(to, a, b, start=(n == 0), stop=(n == 3 * len(terms) - 1))
                        n += 1
                return ins

            def layer_norm_part(n):
                for t in range(NT):
                    pe.wait_ge(s_xn, NT * n + t + 1)
                    if t >= 2:
                        pe.wait_ge(s_xlo, NT * n + t - 1)
                    for k in range(KD):
                        ins = pe.transpose(ps[:, 5 + t % 2, k * P:(k + 1) * P], xn[:, t % 2, k * P:(k + 1) * P],
                                           ident[:, :])
                    ins.then_inc(s_xT, 1)

            pe.wait_ge(s_const, 5)
            layer_norm_part(0)
            pe.wait_ge(s_sum, 1)
            pe.matmul(ps[:, 7, 0:2 * NT], before[0:EP, :], part_sum[0:EP, :, :].rearrange("p l b -> p (l b)"),
                      start=True, stop=True)
            pe.matmul(ps[:, 7, 16:16 + 2 * NT], ones[0:EP, 0:P], part_sum[0:EP, :, :].rearrange("p l b -> p (l b)"),
                      start=True, stop=True).then_inc(s_pre, 1)
            pe.wait_ge(s_bank, 1)

            def sum_chunk(slot, hot, of, n_gathered, n_hot):
                pe.wait_ge(s_gat[slot], n_gathered)
                pe.wait_ge(s_dhot, n_hot)
                l, j, tile = of
                for part_at in range(2):
                    pe.matmul(ps_flat[:, bass.ds(tile * D, D)], dest_hot[:, hot, :],
                              gathered[:, slot, part_at * D:(part_at + 1) * D], start=False, stop=True,
                              skip_group_check=True)
                pe.matmul(ps_flat[:, bass.ds(tile * (2 * RELS) + (7 * 512 + COUNTS + RELS * l), RELS)],
                          dest_hot[:, hot, :], rel_hot[:, l, bass.ds(j, 1), :].rearrange("p a r -> p (a r)"),
                          start=False, stop=True, skip_group_check=True).then_inc(s_seg, 1)

            def tiles_of(l, j, n):
                _, tiles = nc.values_load_multi_w_load_instructions(
                    bank_i[0:1, l, bass.ds(j, n)], engines=[mybir.EngineType.PE], min_val=0, max_val=NT - 1)
                return [(l, j + u, tile) for u, tile in enumerate(tiles)]

            def relation(r, q, first, second, i=None):
                for t in range(NT):
                    if t == 0:
                        pe.wait_ge(s_wlo, 2 * r + 2)
                    if first and t < 2:
                        pe.wait_ge(s_xlo, NT)
                    else:
                        pe.wait_ge(s_rlo, NT * r + t - 1)
                    w = lambda k: 2 * q + k // 2
                    product(ps[:, 5 + (q + t) % 2, :],
                            lambda k: (xT_hi[:, k, t * P:(t + 1) * P], xT_lo[:, k, t * P:(t + 1) * P]),
                            lambda k: (w_hi[:, w(k), (k % 2) * D:(k % 2 + 1) * D],
                                       w_lo[:, w(k), (k % 2) * D:(k % 2 + 1) * D]),
                            range(KD)).then_inc(s_tr, 1)
                    for u in range(COLS_PER_TILE):
                        s = COLS_PER_TILE * t + u
                        pe.wait_ge(s_hot, COLS_PER_REL * r + s + 1)
                        pe.matmul(ps[:, 7, 0:2 * EDGE_CHUNKS], sort_hot[0:EP, s, 0:P],
                                  sort_hot[0:EP, s, P:P + 2 * EDGE_CHUNKS],
                                  start=False, stop=True, skip_group_check=True).then_inc(s_sorted, 1)
                    if second:
                        first_chunk = COLS_PER_REL * r + (COLS_PER_TILE * t - RELS * COLS_PER_REL)
                        s0 = COLS_PER_REL * q + COLS_PER_TILE * t
                        for u, of in enumerate(tiles_of(0, first_chunk, COLS_PER_TILE)):
                            sum_chunk((s0 + u) % RING, s0 + u, of,
                                      32 * i + 16 * (q - RELS + 1), first_chunk + u + 1)

            pe.matmul(ps[:, 7, :], zeros[:, 0:P], zeros[:, :], start=True, stop=True)
            relation(0, 0, True, False)
            relation(1, 1, False, False)
            with pe.Fori(1, RELS // 2) as i:
                relation(2 * i, 0, False, False)
                relation(2 * i + 1, 1, False, False)
            pe.wait_ge(s_dec, 1)
            for t in (*range(NT), 7):
                pe.matmul(ps[:, t, :], zeros[:, 0:P], zeros[:, :], start=True, stop=True)
            half = RELS // 2
            relation(RELS, 0, False, True, half)
            relation(RELS + 1, 1, False, True, half)
            with pe.Fori(half + 1, RELS) as i:
                relation(2 * i, 0, False, True, i)
                relation(2 * i + 1, 1, False, True, i)
            sum_chunk(RING, SEG, tiles_of(0, EDGE_CHUNKS - 1, 1)[0], 16, EDGE_CHUNKS)
            pe.wait_ge(s_wlo, GNN_CHUNKS)
            for t in range(NT):
                if t < 2:
                    pe.wait_ge(s_rlo, 2 * RELS * NT)
                else:
                    pe.wait_ge(s_self, t - 1)
                product(ps[:, 5 + t % 2, :],
                        lambda k: (xT_hi[:, k, t * P:(t + 1) * P], xT_lo[:, k, t * P:(t + 1) * P]),
                        lambda k: (w_hi[:, k // 2, (k % 2) * D:(k % 2 + 1) * D],
                                   w_lo[:, k // 2, (k % 2) * D:(k % 2 + 1) * D]),
                        range(KD)).then_inc(s_tr, 1)
            turns = EDGE_CHUNKS // RING
            with pe.Fori(0, 4) as i:
                for g in range(0, SEG, 4):
                    for s, of in enumerate(tiles_of(1, SEG * i + g, 4), g):
                        sum_chunk(s % RING, s, of, 32 * i + 16 * (turns + s // RING + 1),
                                  SEG * i + (EDGE_CHUNKS + s + 1))
            sum_chunk(RING, SEG, tiles_of(1, EDGE_CHUNKS - 1, 1)[0], 32, 2 * EDGE_CHUNKS)

            pe.wait_ge(s_self, NT)
            pe.wait_ge(s_cnt, 1)
            for t in range(NT):
                to = ps[0:2 * RELS, 5, t * P:(t + 1) * P] if t < 4 else ps[0:2 * RELS, 6, 0:P]
                ins = pe.transpose(to, count[:, t, :], ident[:, :])
            ins.then_inc(s_cntt, 1)
            pe.wait_ge(s_cntc, 1)
            pe.wait_ge(s_brel, 16)
            for t in range(NT):
                ins = pe.matmul(ps[:, t, :], countT[:, t * P:(t + 1) * P], b_rel_sb[:, :], start=False, stop=True,
                                skip_group_check=True)
            ins.then_inc(s_bsum, 1)
            layer_norm_part(1)
            pe.wait_ge(s_xlo, 2 * NT)
            pe.wait_ge(s_rwl, 1)
            pe.wait_ge(s_dec, 2)
            for t in range(NT):
                ins = product(ps[:, 7, t * EXPERTS:(t + 1) * EXPERTS],
                              lambda k: (xT_hi[:, k, t * P:(t + 1) * P], xT_lo[:, k, t * P:(t + 1) * P]),
                              lambda k: (rw_hi[:, k * EXPERTS:(k + 1) * EXPERTS],
                                         rw_lo[:, k * EXPERTS:(k + 1) * EXPERTS]),
                              range(KD))
            ins.then_inc(s_lg, 1)
            pe.wait_ge(s_cw, 1)
            for t in range(NT):
                to = ps[0:EXPERTS, 6, t * P:(t + 1) * P] if t < 4 else ps[0:EXPERTS, 7, 128:256]
                ins = pe.transpose(to, cw[:, t, :], ident[:, :])
                if t >= 3:
                    ins.then_inc(s_cwt, 1)
            pe.wait_ge(s_cwc, 1)
            for t in range(NT):
                if t == 4:
                    pe.wait_ge(s_comb, 1)
                pe.matmul(ps[:, 4 + t % 4, :], cwT[:, t * P:(t + 1) * P], b2[:, :], start=True, stop=True)\
                    .then_inc(s_b2, 1)
            pe.wait_ge(s_wlo, GNN_CHUNKS + KH)

            def expert(e, last):
                for j in range(KH):
                    n = fc1_order(j) - (SLOTS - KH)
                    pe.wait_ge(s_wlo, SLOTS * e + (GNN_CHUNKS + n + 1))
                    for c in range(2):
                        pe.wait_ge(s_free1, 16 * e + 2 * j + c + 1)
                        for half_at in range(2):
                            ins = product(
                                ps[:, 2 * c + half_at, 0:TOK],
                                lambda k: (w_hi[:, j, (2 * k + half_at) * P:(2 * k + half_at + 1) * P],
                                           w_lo[:, j, (2 * k + half_at) * P:(2 * k + half_at + 1) * P]),
                                lambda k: (xT_hi[:, k, c * TOK:(c + 1) * TOK], xT_lo[:, k, c * TOK:(c + 1) * TOK]),
                                range(KD))
                        ins.then_inc(s_fc1, 1)
                for t in range(NT):
                    pe.wait_ge(s_comb, NT * e + (5, 2, 3, 4, 6)[t])
                    m = 0
                    for k in range(KH):
                        if t == 0:
                            pe.wait_ge(s_alo, 16 * e + 2 * k + 2)
                            if k % 2 == 0:
                                pe.wait_ge(s_wlo, SLOTS * e + (GNN_CHUNKS + KH + (k // 2 if last else k) + 1))
                        a_h, a_l = (a[:, k, t * P:(t + 1) * P] for a in (aT_hi, aT_lo))
                        b_h, b_l = (b[:, KH + k // 2, (k % 2) * D:(k % 2 + 1) * D] for b in (w_hi, w_lo))
                        for a, b in ((a_h, b_h), (a_h, b_l), (a_l, b_h)):
                            ins = pe.matmul(ps[:, 4 + t % 4, :], a, b, start=(m == 0), stop=(m == 3 * KH - 1))
                            m += 1
                    ins.then_inc(s_fc2, 1)

            with pe.Fori(0, EXPERTS - 1) as e:
                expert(e, False)
            last_expert(expert)


def last_expert(expert):
    expert(EXPERTS - 1, True)


def kernel(x, src, dst, edge_type_8, L0_gnn_W_self, L0_gnn_b_self, L0_gnn_W_rel, L0_gnn_b_rel,
           L0_ffn_router_w, L0_ffn_router_b, L0_ffn_fc1_w, L0_ffn_fc1_b, L0_ffn_fc2_w, L0_ffn_fc2_b):
    import numpy as np
    import concourse.bacc as bacc
    from concourse.bass_utils import run_bass_kernel_spmd

    gnn = np.concatenate([np.asarray(L0_gnn_W_rel), np.asarray(L0_gnn_W_self)[None]])
    gnn = gnn.transpose(0, 2, 1).reshape(2 * RELS + 1, 2, 2, P, D).transpose(0, 1, 3, 2, 4)
    gnn = gnn.reshape(GNN_CHUNKS, P, CH)
    fc1 = np.asarray(L0_ffn_fc1_w).reshape(EXPERTS, 2, KH, P, KD, P).transpose(0, 2, 5, 4, 1, 3)
    fc1 = fc1.reshape(EXPERTS, KH, P, CH)
    fc2 = np.asarray(L0_ffn_fc2_w).transpose(0, 2, 1).reshape(EXPERTS, 4, 2, P, D).transpose(0, 1, 3, 2, 4)
    fc2 = fc2.reshape(EXPERTS, 4, P, CH)
    stream = [fc1[0, j] for j in range(KH)]
    for e in range(EXPERTS):
        for j in range(KH):
            if j < 4:
                stream.append(fc2[e, j])
            if e + 1 < EXPERTS:
                stream.append(fc1[e + 1, j])
    named = {
        "x": x, "src": src, "dst": dst, "rel": edge_type_8, "gnn_w": gnn,
        "b_self": np.asarray(L0_gnn_b_self)[None], "b_rel": L0_gnn_b_rel,
        "router_w": np.asarray(L0_ffn_router_w).reshape(EXPERTS, KD, P).transpose(2, 1, 0).reshape(P, KD * EXPERTS),
        "router_b": np.asarray(L0_ffn_router_b)[None],
        "ffn_w": np.stack(stream),
        "fc1_b": np.asarray(L0_ffn_fc1_b).reshape(EXPERTS * 2 * KH, P).transpose(1, 0),
        "fc2_b": L0_ffn_fc2_b,
    }
    nc = bacc.Bacc("TRN2", target_bir_lowering=False, num_devices=1)
    arrays, args = {}, []
    for name, a in named.items():
        a = np.ascontiguousarray(a)
        arrays[f"in_{name}"] = a
        args.append(nc.dram_tensor(f"in_{name}", a.shape, mybir.dt.from_np(a.dtype), kind="ExternalInput").ap())
    args.append(nc.dram_tensor("out_x", (NODES, D), F32, kind="ExternalOutput").ap())
    build(nc, *args)
    return run_bass_kernel_spmd(nc, [arrays], core_ids=[0]).results[0]["out_x"]
```

```python
from contextlib import ExitStack

import concourse.bass as bass
from concourse import mybir

F32 = mybir.dt.float32
F16 = mybir.dt.float16
I32 = mybir.dt.int32
U32 = mybir.dt.uint32
ACT = mybir.ActivationFunctionType
ALU = mybir.AluOpType
AX_X = mybir.AxisListType.X

P = 128
NODES = 625
D = 512
KD = D // P
NT = (NODES + P - 1) // P
PADDED = NT * P
LAST = NODES - (NT - 1) * P
EDGES = 20000
RELS = 8
EXPERTS = 8
HID = 1024
KH = HID // P

EP = 125
EC = EDGES // EP
EDGE_CHUNKS = (EDGES + NT * (P - 1)) // P
COLS_PER_REL = EC // RELS
COLS_PER_TILE = COLS_PER_REL // NT
RING = 20
HALF = RING // 2
SEG = 2 * COLS_PER_REL
TAIL = EDGE_CHUNKS - 4 * SEG
assert TAIL == 1 and SEG == 2 * RING

CH = 1024
REL_CHUNKS = 2
GNN_CHUNKS = REL_CHUNKS * (2 * RELS + 1)
SLOTS = 12
COUNTS = 400
GNN_RAW = 4
RAW = 6
GROUPS = ((0, 1, 2), (3, 4, 5), (6, 7))
GROUP_BANKS = ((2, 3), (4, 5), (7, 1))
CUTS = (4, 7, 7, 12)
PASSES = (2 * NODES + EXPERTS * P) // P

BIAS_ROWS = 80
BIAS2_BANKS = (2, 3, 4, 5, 7)

SX = 64.0
SW = 64.0
SH = 64.0
SA = 16.0
LN_EPS = 1e-5


def build(nc, x, src, dst, rel, gnn_w, b_self, b_rel, router_w, router_b, ffn_w, fc1_b, fc2_b, out):
    with ExitStack() as ctx:
        def sb(name, shape, dt):
            return ctx.enter_context(nc.sbuf_tensor(name, shape, dt))

        def sem(name):
            return ctx.enter_context(nc.semaphore(name))

        x_sb = sb("x_sb", [P, NT, D], F32)
        xT_hi = sb("xT_hi", [P, KD, PADDED], F16)
        xT_lo = sb("xT_lo", [P, KD, PADDED], F16)
        w_raw = sb("w_raw", [P, GNN_RAW, CH], F32)
        edge_mem = sb("edge_mem", [P, RAW - GNN_RAW, CH], F32)

        def raw_slot(n):
            return w_raw[:, n, :] if n < GNN_RAW else edge_mem[:, n - GNN_RAW, :]

        pos_lo = edge_mem[:, 0, 0:2 * EC]
        pos_hi = edge_mem[:, 0, 2 * EC:4 * EC]
        packed_pair = edge_mem[:, 0, 4 * EC:6 * EC]
        packed = packed_pair.bitcast(F16).rearrange("p (l c v) -> p l c v", l=2, v=2)
        iota_i = edge_mem[:, 1, 0:176].bitcast(I32)
        code_i = edge_mem[:, 1, 0:EDGE_CHUNKS].bitcast(I32)
        part_i = edge_mem[:, 1, EDGE_CHUNKS:3 * EDGE_CHUNKS].bitcast(I32).rearrange("p (v c) -> p v c", v=2)
        row_rel = edge_mem[:, 1, 3 * EDGE_CHUNKS:4 * EDGE_CHUNKS]
        bank_f = edge_mem[0:1, 1, 4 * EDGE_CHUNKS:6 * EDGE_CHUNKS].rearrange("p (l c) -> p l c", l=2)
        w_hi = sb("w_hi", [P, SLOTS, CH], F16)
        w_lo = sb("w_lo", [P, SLOTS, CH], F16)

        def self_sb(t):
            return (w_hi[:, KH + t, :] if t < 4 else w_lo[:, KH, :]).bitcast(F32)

        scratch = sb("scratch", [P, 2 * NT * 1024 + (RING + 1) * 1024 + 20 * 456 + (SEG + 1) * P], F16)
        cut = [0]

        def part(cols):
            cut[0] += cols
            return scratch[:, cut[0] - cols:cut[0]]

        rows_out = part(2 * NT * 1024).rearrange("p (q t c) -> p q t c", q=2, t=NT)
        gathered = part((RING + 1) * 1024).rearrange("p (s c) -> p s c", c=1024)
        sort_hot = part(20 * 456).rearrange("p (s c) -> p s c", c=456)
        bias_mem = sort_hot.rearrange("p s c -> p (s c)")
        countT = bias_mem[0:BIAS_ROWS, 0:PADDED]
        b_parts = bias_mem[0:BIAS_ROWS, PADDED:PADDED + D]
        count = bias_mem[:, 2 * PADDED:2 * PADDED + 2 * NT * BIAS_ROWS].bitcast(F32)\
            .rearrange("p (t r) -> p t r", t=NT)
        count_hi = bias_mem[:, PADDED + D:PADDED + D + NT * 2 * RELS].rearrange("p (t r) -> p t r", t=NT)
        dest_hot = part((SEG + 1) * P).rearrange("p (s c) -> p s c", c=P)
        cut[0] = 2 * NT * 1024

        def edge_part(rows, dt):
            return part(2 * rows * EC).bitcast(dt).rearrange("p (n c) -> p n c", c=EC)

        edge_in = edge_part(3, I32)
        edge_t = edge_part(2, I32)
        edge_l = edge_part(2, I32)
        tile_f = edge_part(2, F32)
        place = edge_part(2, F32)
        place_i = edge_part(2, I32)
        lo_i = edge_part(2, I32)
        rel_f = edge_part(1, F32)[:, 0, :]
        in_bucket = edge_part(2 * NT, F32).rearrange("p (l b) c -> p l b c", l=2)
        running = edge_part(2 * NT, F32).rearrange("p (l b) c -> p l b c", l=2)
        assert cut[0] <= 2 * NT * 1024 + (RING + 1) * 1024
        cut[0] = 0
        w_hi2 = part(SLOTS * CH).rearrange("p (s c) -> p s c", s=SLOTS)
        w_lo2 = part(SLOTS * CH).rearrange("p (s c) -> p s c", s=SLOTS)
        wset = ((w_hi, w_lo), (w_hi2, w_lo2))
        xr_hi = part(NT * D).rearrange("p (t n) -> p t n", t=NT)
        xr_lo = part(NT * D).rearrange("p (t n) -> p t n", t=NT)
        slot_hot = part(NT * P).rearrange("p (t n) -> p t n", t=NT)
        xg_hi = part(KD * P).rearrange("p (k n) -> p k n", k=KD)
        xg_lo = part(KD * P).rearrange("p (k n) -> p k n", k=KD)
        aT_hi = part(KH * P).rearrange("p (k n) -> p k n", k=KH)
        aT_lo = part(KH * P).rearrange("p (k n) -> p k n", k=KH)
        silu = part(2 * KH * P).bitcast(F32).rearrange("p (k n) -> p k n", k=KH)
        glu = part(2 * KH * P).bitcast(F32).rearrange("p (k n) -> p k n", k=KH)
        acc = part(2 * NT * D).bitcast(F32).rearrange("p (t n) -> p t n", t=NT)
        y_sb = part(2 * D).bitcast(F32)

        def xn_of(n, t):
            return xn[:, t % 2, :] if n == 0 else acc[:, t, :]

        cwT = part(2 * PADDED).bitcast(F32)[0:EXPERTS, :]
        in_pass = part(2 * (NT + 1) * EXPERTS * NT).bitcast(F32)\
            .rearrange("p (c e t) -> p c e t", c=NT + 1, e=EXPERTS)

        xn = sb("xn", [P, 2, D], F32)
        main_hot = [xn[:, n, 0:NT * P // 2].bitcast(F16).rearrange("p (t n) -> p t n", t=NT) for n in range(2)]
        b_rel_sb = sb("b_rel_sb", [BIAS_ROWS, D], F32)
        rel_hot = sb("rel_hot", [P, 2, EDGE_CHUNKS, RELS], F16)
        b_self_row = w_lo[:, KH + 1, :].bitcast(F32)
        ident = sb("ident", [P, P], F32)
        zeros = sb("zeros", [P, D], F16)
        iota_f = sb("iota_f", [P, 176], F32)
        iota_h = sb("iota_h", [P, 176], F16)
        before = sb("before", [P, P], F32)
        ones = sb("ones", [P, EC], F32)
        stats = sb("stats", [P, NT, 6], F32)
        mv = sb("mv", [P, NT, 2], F32)
        rstd = sb("rstd", [P, NT], F32)
        std = sb("std", [P, NT], F32)
        part_sum = sb("part_sum", [P, 2, NT], F32)
        pad_i = sb("pad_i", [P, 2, NT], I32)
        pad_f = sb("pad_f", [P, 2, NT], F32)
        pad_end = sb("pad_end", [P, 2, NT], F32)
        pad_base = sb("pad_base", [P, 2, NT], F32)
        offset = sb("offset", [P, 2, NT], F32)
        bank_i = sb("bank_i", [1, 2, EDGE_CHUNKS + 3], I32)
        dest_f = sb("dest_f", [P, 2, EDGE_CHUNKS], F32)
        row_idx = sb("row_idx", [P, 2, EDGE_CHUNKS], U32)
        ring_idx = sb("ring_idx", [P, RING + 1], U32)
        rw_raw = sb("rw_raw", [P, KD * EXPERTS], F32)
        rw_hi = sb("rw_hi", [P, KD * EXPERTS], F16)
        rw_lo = sb("rw_lo", [P, KD * EXPERTS], F16)
        rb_row = sb("rb_row", [P, EXPERTS], F32)
        logits = sb("logits", [P, NT, EXPERTS], F32)
        top = sb("top", [P, NT, 8], F32)
        top_i = sb("top_i", [P, NT, 8], U32)
        top_if = sb("top_if", [P, NT, 8], F32)
        soft = sb("soft", [P, 4, NT], F32)
        valid = sb("valid", [P, NT], F32)
        hot1 = sb("hot1", [P, NT, EXPERTS], F32)
        hot2 = sb("hot2", [P, NT, EXPERTS], F32)
        mask = sb("mask", [P, NT, EXPERTS], F32)
        cum = sb("cum", [P, NT, EXPERTS], F32)
        pos = sb("pos", [P, NT, EXPERTS], F32)
        cw_a = sb("cw_a", [P, NT, EXPERTS], F32)
        cw = sb("cw", [P, NT, EXPERTS], F32)
        np_f = sb("np_f", [P, EXPERTS], F32)
        np_i = sb("np_i", [P, EXPERTS], I32)
        end_f = sb("end_f", [P, EXPERTS], F32)
        first_f = sb("first_f", [P, EXPERTS], F32)
        plan_i = sb("plan_i", [1, EXPERTS, 2], I32)
        warm = sb("warm", [1, 1], F32)
        slot_column = sb("slot_column", [P, 2, NT], F32)
        y_row = sb("y_row", [P, 2, NT], F32)
        y_idx = sb("y_idx", [P, 2, NT], U32)
        b1 = sb("b1", [P, EXPERTS * 2 * KH], F32)
        b1_s = sb("b1_s", [P, EXPERTS * 2 * KH], F32)
        b2 = sb("b2", [EXPERTS, D], F32)
        ps = ctx.enter_context(nc.psum_tensor("ps", [P, 8, 512], F32))
        ps_flat = ps[:, :, :].rearrange("p b n -> p (b n)")
        rows_dram = nc.dram_tensor("rows_dram", [2 * RELS * PADDED, 2 * D], F16, kind="Internal").ap()
        y_dram = nc.dram_tensor("y_dram", [(PASSES + NT - 1) * P, D], F32, kind="Internal").ap()
        rows_by_rel = rows_dram.rearrange("(r t p) c -> p r t c", p=P, t=NT)

        s_x = sem("x_loaded")
        s_xpad = sem("x_pad_zeroed")
        s_edges = sem("edges_loaded")
        s_small = sem("small_loaded")
        s_raw = [sem(f"w_raw_loaded{s}") for s in range(RAW)]
        s_const = sem("consts_ready")
        s_pool = sem("pool_chain")
        s_dve = sem("dve_chain")
        s_var = sem("var_ready")
        s_std = sem("std_ready")
        s_xn = sem("xn_ready")
        s_xT = sem("xn_transposed")
        s_xhi = sem("xT_hi_ready")
        s_xlo = sem("xT_lo_ready")
        s_whi = sem("w_hi_ready")
        s_wlo = sem("w_lo_ready")
        s_sum = sem("part_sum_ready")
        s_pre = sem("prefix_done")
        s_bank = sem("bank_table_ready")
        s_hot = sem("sort_hot_ready")
        s_sorted = sem("column_sorted")
        s_dec = sem("list_decoded")
        s_tr = sem("transformed")
        s_brel = sem("b_rel_loaded")
        s_cnt = sem("counts_ready")
        s_cntt = sem("counts_transposed")
        s_cntc = sem("countT_copied")
        s_bsum = sem("biases_summed")
        s_rhi = sem("row_hi_ready")
        s_rlo = sem("row_lo_ready")
        s_store = [sem(f"rows_stored{q}") for q in range(2)]
        s_idx = sem("idx_copied")
        s_gat = [sem(f"gathered{s}") for s in range(RING + 1)]
        s_dhot = sem("dest_hot_ready")
        s_seg = sem("chunk_summed")
        s_self = sem("self_evacuated")
        s_lg = sem("logits_ready")
        s_dif = sem("top_diff_ready")
        s_exp = sem("top_exp_ready")
        s_cw = sem("cw_ready")
        s_cwt = sem("cw_transposed")
        s_cwc = sem("cwT_copied")
        s_b2 = sem("bias2_summed")
        s_acc = sem("acc_started")
        s_cum = sem("expert_counts_ready")
        s_epre = sem("expert_prefix_done")
        s_plan = sem("passes_planned")
        s_xs = sem("xn_scaled")
        s_xrh = sem("xr_hi_ready")
        s_xrl = sem("xr_lo_ready")
        s_slot = sem("slot_hot_ready")
        s_mslot = sem("main_hot_ready")
        s_mcol = sem("main_columns_copied")
        s_col = sem("columns_copied")
        s_disph = sem("tokens_hi_brought")
        s_disp = sem("tokens_brought")
        s_xgh = sem("xg_hi_ready")
        s_xgl = sem("xg_lo_ready")
        s_fc1 = sem("fc1_group_done")
        s_silu = sem("silu_ready")
        s_glu = sem("glu_ready")
        s_ahi = sem("a_hi_ready")
        s_alo = sem("a_lo_ready")
        s_fc2 = sem("fc2_done")
        s_y = sem("y_ready")
        s_yst = sem("y_stored")
        s_yfree = sem("y_free")
        s_turn = sem("turn")
        s_yzero = sem("y_dram_zeroed")
        s_ygat = [sem(f"y_gathered{t}") for t in range(NT)]
        s_done = sem("tile_done")
        s_half = sem("first_row_added")
        s_rwh = sem("router_hi_ready")
        s_rwl = sem("router_lo_ready")
        s_out = sem("out_stored")

        block = ctx.enter_context(nc.Block())

        def pairs(eng, expert):
            with eng.Fori(0, EXPERTS // 2 - 1) as i:
                expert(2 * i, 0, False)
                expert(2 * i + 1, 1, False)
            expert(EXPERTS - 2, 0, False)
            expert(EXPERTS - 1, 1, True)

        def chunks_in_pass(e, parity, last, main):
            own = [(e, n, parity) for n in range(KH, SLOTS)]
            chunks = [] if not main else own if last else own + [(e + 1, n, 1 - parity) for n in range(KH)]
            edges = (0, *CUTS, SLOTS)
            return [chunks[a:b] for a, b in zip(edges, edges[1:])]

        def plan_of(kind, e):
            _, (first, count) = nc.values_load_multi_w_load_instructions(
                plan_i[0:1, bass.ds(e, 1), :].rearrange("p e n -> p (e n)"), engines=[kind],
                min_val=0, max_val=PASSES - 1)
            return first, count

        def passes(eng, kind, e, do):
            first, count = plan_of(kind, e)
            do(e, 0, first, True)
            with eng.If(count > 1):
                with eng.Fori(1, NT) as c:
                    with eng.If(count > c):
                        do(e, c, first + c, False)

        @block.sync
        def _(sp):
            for n, a in enumerate((src, dst, rel)):
                sp.dma_start(edge_in[0:EP, n, :], a.rearrange("(p c) -> p c", c=EC)).then_inc(s_edges, 16)
            sp.dma_start(x_sb[:, 0:NT - 1, :],
                         x[0:(NT - 1) * P, :].rearrange("(t p) d -> p t d", p=P)).then_inc(s_x, 16)
            sp.wait_ge(s_xpad, 1)
            sp.dma_start(x_sb[0:LAST - 1, NT - 1, :], x[(NT - 1) * P:NODES - 1, :]).then_inc(s_x, 16)
            sp.dma_start(x_sb[LAST - 1:LAST, NT - 1, :], x[NODES - 1:NODES, :]).then_inc(s_x, 16)

            def load_gnn(chunk, slot):
                sp.dma_start(w_raw[:, slot, :], gnn_w[bass.ds(chunk, 1), :, :].rearrange("a p c -> p (a c)"))\
                    .then_inc(s_raw[slot], 16)

            load_gnn(0, 0)
            load_gnn(1, 1)
            for n in range(3):
                sp.dma_start(b_rel_sb[32 * n:32 * n + 2 * RELS, :], b_rel).then_inc(s_brel, 16)
            sp.wait_ge(s_const, 4)
            for n in range(2):
                sp.dma_start(y_dram[0:PASSES * P, :].rearrange("(t p) c -> p t c", p=P)[:, :, n * D // 2:(n + 1) * D // 2],
                             zeros[:, :].bitcast(F32).rearrange("p (a c) -> p a c", a=1)
                             .to_broadcast([P, PASSES, D // 2])).then_inc(s_yzero, 16)
            sp.dma_start(b_self_row[:, :], b_self.to_broadcast([P, D])).then_inc(s_small, 16)
            sp.dma_start(rw_raw[:, :], router_w).then_inc(s_small, 16)
            sp.dma_start(rb_row[:, :], router_b.to_broadcast([P, EXPERTS])).then_inc(s_small, 16)
            sp.dma_start(b1[:, :], fc1_b).then_inc(s_small, 16)
            sp.dma_start(b2[:, :], fc2_b).then_inc(s_small, 16)

            def relation(r, q):
                sp.wait_ge(s_wlo, 2 * r + 2)
                load_gnn(2 * r + 2, 2 * (1 - q))
                load_gnn(2 * r + 3, 2 * (1 - q) + 1)
                sp.wait_ge(s_rlo, NT * (r + 1))
                sp.dma_start(rows_by_rel[:, bass.ds(r, 1), :, :].rearrange("p r t c -> p (r t) c"),
                             rows_out[:, q, :, :]).then_inc(s_store[q], 16)

            with sp.Fori(0, RELS) as i:
                relation(2 * i, 0)
                relation(2 * i + 1, 1)

            def load_ffn(i):
                for n in range(RAW):
                    if isinstance(i, int):
                        sp.wait_ge(s_wlo, GNN_CHUNKS)
                        if n >= GNN_RAW:
                            sp.wait_ge(s_dec, 2)
                    else:
                        sp.wait_ge(s_wlo, RAW * i + (GNN_CHUNKS - RAW + n + 1))
                    sp.dma_start(raw_slot(n),
                                 ffn_w[bass.ds(RAW * i + n, 1), :, :].rearrange("a p c -> p (a c)"))\
                        .then_inc(s_raw[n], 16)

            load_ffn(0)
            with sp.Fori(1, EXPERTS * SLOTS // RAW) as i:
                load_ffn(i)
            for t in range(NT):
                sp.wait_ge(s_done, t + 1)
                if t < NT - 1:
                    sp.dma_start(out[t * P:(t + 1) * P, :], acc[:, t, :]).then_inc(s_out, 16)
                else:
                    sp.dma_start(out[t * P:NODES - 1, :], acc[0:LAST - 1, t, :]).then_inc(s_out, 16)
                    sp.dma_start(out[NODES - 1:NODES, :], acc[LAST - 1:LAST, t, :]).then_inc(s_out, 16)
            sp.wait_ge(s_store[0], 16 * RELS)
            sp.wait_ge(s_store[1], 16 * RELS)
            sp.wait_ge(s_out, 16 * (NT + 1))

        @block.gpsimd
        def _(pool):
            links = [0]

            def link(ins):
                links[0] += 1
                ins.then_inc(s_pool, 1)
                pool.wait_ge(s_pool, links[0])

            link(pool.memset(ident[:, :], 0.0))
            pool.affine_select(out=ident[:, :], in_=ident[:, :], compare_op=ALU.not_equal, fill=1.0, base=0,
                               pattern=[[-1, P]], channel_multiplier=1).then_inc(s_const, 1)
            link(pool.memset(before[:, :], 0.0))
            pool.affine_select(out=before[:, :], in_=before[:, :], compare_op=ALU.is_ge, fill=1.0, base=0,
                               pattern=[[-1, P]], channel_multiplier=1).then_inc(s_const, 1)
            link(pool.iota(iota_i, pattern=[[1, 176]], base=0, channel_multiplier=0))
            link(pool.tensor_copy(iota_f[:, :], iota_i))
            pool.tensor_copy(iota_h[:, :], iota_f[:, :]).then_inc(s_const, 1)
            pool.memset(zeros[:, :], 0.0).then_inc(s_const, 1)
            pool.memset(ones[:, :], 1.0).then_inc(s_const, 1)
            link(pool.memset(valid[:, :], 1.0))
            pool.affine_select(out=valid[:, :], in_=valid[:, :], compare_op=ALU.is_ge, fill=0.0, base=NODES - 1,
                               pattern=[[-P, NT]], channel_multiplier=-1).then_inc(s_const, 1)

            def gather(l, slot):
                pool.indirect_dma_start(gathered[:, slot, :], None, rows_dram[0:(l + 1) * RELS * PADDED, :],
                                        bass.IndirectOffsetOnAxis(ap=ring_idx[:, slot:slot + 1], axis=0))\
                    .then_inc(s_gat[slot], 16)

            def gather_half(l, a, h, batch, summed):
                if summed is not None:
                    pool.wait_ge(s_seg, summed)
                    pool.sem_inc(s_idx, 1)
                at = l * EDGE_CHUNKS + RING * a + HALF * h
                pool.tensor_copy(ring_idx[:, HALF * h:HALF * h + HALF],
                                 row_idx[:, :, :].rearrange("p l c -> p (l c)")[:, bass.ds(at, HALF)])\
                    .then_inc(s_idx, 1)
                pool.wait_ge(s_idx, batch)
                pool.sem_inc(s_pool, 1)
                for s in range(HALF * h, HALF * h + HALF):
                    gather(l, s)

            turns = EDGE_CHUNKS // RING
            for l in range(2):
                pool.wait_ge(s_dec, l + 1)
                for q in range(2):
                    pool.wait_ge(s_store[q], 16 * (RELS // 2) * (l + 1))
                base = l * (4 * turns - 2 + 1)
                for h in range(2):
                    gather_half(l, 0, h, base + (h + 1) * (1 + l), None if l == 0 else
                                EDGE_CHUNKS - TAIL - RING + HALF * (h + 1))
                first = base + 2 * (1 + l)
                with pool.Fori(1, turns) as a:
                    for h in range(2):
                        gather_half(l, a, h, 4 * a + (first - 4 + 2 * (h + 1)),
                                    RING * a + (l * EDGE_CHUNKS - RING + HALF * (h + 1)))
                if l == 1:
                    pool.wait_ge(s_seg, EDGE_CHUNKS)
                pool.tensor_copy(ring_idx[:, RING:RING + 1],
                                 row_idx[:, l, EDGE_CHUNKS - 1:EDGE_CHUNKS]).then_inc(s_idx, 1)
                pool.wait_ge(s_idx, first + 4 * (turns - 1) + 1)
                gather(l, RING)

            for t in range(NT):
                pool.wait_ge(s_xs, t + 1)
                pool.tensor_tensor(xr_lo[:, t, :], xn_of(1, t), xr_hi[:, t, :], ALU.subtract).then_inc(s_xrl, 1)
            pool.wait_ge(s_yzero, 32)
            pool.wait_ge(s_plan, 1)
            pool.sem_inc(s_yfree, 1)

            def slots(to, c, e, n, s_column, s_made, made):
                pool.tensor_copy(slot_column[:, n, :],
                                 in_pass.rearrange("p c e t -> p (c e t)")
                                 [:, bass.ds(NT * EXPERTS * c + NT * e, NT)]).then_inc(s_column, 1)
                pool.wait_ge(s_column, made)
                pool.sem_inc(s_pool, 1)
                for t in range(NT):
                    ins = pool.tensor_scalar(to[:, t, :], iota_h[:, 0:P], slot_column[:, n, t:t + 1],
                                             None, ALU.is_equal)
                ins.then_inc(s_made, 1)

            def expert(e, parity, last):
                def one(e, c, q, main):
                    pool.wait_ge(s_disp, q + 2)
                    pool.sem_inc(s_pool, 1)
                    if main and not last:
                        slots(main_hot[1 - parity], 0, e + 1, 0, s_mcol, s_mslot, e + 1)
                    slots(slot_hot, c + 1, e, 1, s_col, s_slot, q + 1)
                    pool.wait_ge(s_slot, q + 1)
                    pool.wait_ge(s_y, q + 2)
                    pool.sem_inc(s_pool, 1)
                    pool.dma_start(y_dram[bass.ds(q * P, P), :], y_sb).then_inc(s_yst, 16)
                    pool.wait_ge(s_yst, 16 * q + 16)
                    pool.sem_inc(s_yfree, 1)

                passes(pool, mybir.EngineType.Pool, e, one)

            pairs(pool, expert)
            pool.wait_ge(s_wlo, GNN_CHUNKS + EXPERTS * SLOTS)
            for t in range(NT):
                for n in range(2):
                    if t == GNN_RAW and n == 0:
                        pool.wait_ge(s_done, 1)
                    pool.indirect_dma_start(w_raw[:, t % GNN_RAW, n * D:(n + 1) * D], None, y_dram[0:PASSES * P, :],
                                            bass.IndirectOffsetOnAxis(ap=y_idx[:, n, t:t + 1], axis=0))\
                        .then_inc(s_ygat[t], 16)

        @block.scalar
        def _(act):
            def split_hi(slot, raw, loaded, to=w_hi):
                act.wait_ge(s_raw[raw], loaded)
                act.activation(to[:, slot, :], raw_slot(raw), ACT.Copy, scale=SW).then_inc(s_whi, 1)

            def layer_norm_part(n):
                act.wait_ge(s_var, n + 1)
                act.activation(std[:, :], rstd[:, :], ACT.Sqrt).then_inc(s_std, 1)
                for t in range(NT):
                    act.wait_ge(s_xT, NT * n + t + 1)
                    act.activation(xT_hi[:, :, t * P:(t + 1) * P],
                                   ps[:, 5 + t % 2, :].rearrange("p (k m) -> p k m", k=KD),
                                   ACT.Copy, scale=SX).then_inc(s_xhi, 1)

            layer_norm_part(0)
            split_hi(0, 0, 16)
            split_hi(1, 1, 16)
            act.wait_ge(s_small, 16 * 5)
            act.activation(rw_hi[:, :], rw_raw[:, :], ACT.Copy, scale=SW).then_inc(s_rwh, 1)

            def relation(r, q, i):
                for t in range(NT):
                    if t >= NT - 2:
                        slot = 2 * (1 - q) + t - (NT - 2)
                        if t == NT - 2 and not (isinstance(r, int) and r == 0):
                            act.wait_ge(s_tr, NT * r)
                        split_hi(slot, slot, 16 * (i + 1) + 16 * q)
                    act.wait_ge(s_tr, NT * r + t + 1)
                    if t == 0 and not (isinstance(i, int) and i == 0):
                        act.wait_ge(s_store[q], 16 * i)
                    act.activation(rows_out[:, q, t, 0:D], ps[:, 5 + (q + t) % 2, :], ACT.Copy,
                                   scale=SH / (SX * SW)).then_inc(s_rhi, 1)

            relation(0, 0, 0)
            relation(1, 1, 0)
            with act.Fori(1, RELS) as i:
                relation(2 * i, 0, i)
                relation(2 * i + 1, 1, i)
            for t in range(NT):
                act.wait_ge(s_tr, 2 * RELS * NT + t + 1)
                act.activation(self_sb(t), ps[:, 5 + t % 2, :], ACT.Copy, scale=1.0 / (SX * SW))\
                    .then_inc(s_self, 1)

            def split_ffn(e, n, parity):
                used = sum(c % GNN_RAW == n % RAW for c in range(GNN_CHUNKS))
                split_hi(n, n % RAW, 16 * (SLOTS // RAW) * e + 16 * (n // RAW + used + 1), wset[parity][0])

            for j in range(KH):
                split_ffn(0, j, 0)
            layer_norm_part(1)
            for t in range(NT):
                act.activation(xr_hi[:, t, :], xn_of(1, t), ACT.Copy, scale=SX).then_inc(s_xrh, 1)
                act.wait_ge(s_xrh, t + 1)
                act.activation(xn_of(1, t), xn_of(1, t), ACT.Copy, scale=SX).then_inc(s_xs, 1)
            act.wait_ge(s_dif, 1)
            act.activation(soft[:, 1, :], soft[:, 0, :], ACT.Exp).then_inc(s_exp, 1)
            act.wait_ge(s_plan, 1)
            act.sem_inc(s_y, 1)

            def expert(e, parity, last):
                if parity == 0:
                    act.activation(warm[0:1, 0:1], zeros[0:1, 0:1], ACT.Silu)

                def one(e, c, q, main):
                    splits = chunks_in_pass(e, parity, last, main)
                    act.wait_ge(s_disph, q + 1)
                    act.activation(xg_hi[:, :, :], ps[:, 0, :].rearrange("p (k n) -> p k n", k=KD), ACT.Copy)\
                        .then_inc(s_xgh, 1)
                    act.wait_ge(s_disp, q + 2)
                    act.activation(xg_lo[:, :, :], ps[:, 1, :].rearrange("p (k n) -> p k n", k=KD), ACT.Copy)\
                        .then_inc(s_xgl, 1)
                    for g, tiles in enumerate(GROUPS):
                        for chunk in splits[g]:
                            split_ffn(*chunk)
                        act.wait_ge(s_fc1, len(GROUPS) * q + g + 1)
                        act.sem_inc(s_turn, 1)
                        for at, j in enumerate(tiles):
                            act.activation(silu[:, j, :], ps[:, GROUP_BANKS[g][0], at * P:(at + 1) * P], ACT.Silu,
                                           bias=b1[:, bass.ds(2 * KH * e + j, 1)], scale=1.0 / (SX * SW))\
                                .then_inc(s_silu, 1)
                        act.wait_ge(s_glu, len(GROUPS) * q + g + 1)
                        act.activation(aT_hi[:, tiles[0]:tiles[-1] + 1, :], glu[:, tiles[0]:tiles[-1] + 1, :],
                                       ACT.Copy, scale=SA / (SX * SW)).then_inc(s_ahi, 1)
                    for chunk in splits[-2]:
                        split_ffn(*chunk)
                    act.wait_ge(s_yfree, q + 1)
                    act.wait_ge(s_fc2, q + 1)
                    act.activation(y_sb, ps[:, 6, :], ACT.Copy, scale=1.0 / (SA * SW)).then_inc(s_y, 1)
                    for chunk in splits[-1]:
                        split_ffn(*chunk)

                passes(act, mybir.EngineType.Activation, e, one)

            pairs(act, expert)

        @block.vector
        def _(dve):
            links = [0]

            def link(ins):
                links[0] += 1
                ins.then_inc(s_dve, 1)
                dve.wait_ge(s_dve, links[0])

            def split_lo(slot, raw, hi_count, hi=w_hi, lo=w_lo):
                dve.wait_ge(s_whi, hi_count)
                dve.scalar_tensor_tensor(out=lo[:, slot, :], in0=raw_slot(raw), scalar=SW,
                                         in1=hi[:, slot, :], op0=ALU.mult, op1=ALU.subtract)\
                    .then_inc(s_wlo, 1)

            def layer_norm_part(n):
                for t in range(NT):
                    if n == 0:
                        if t == 0:
                            dve.wait_ge(s_x, 48)
                    ins = dve.bn_stats(stats[:, t, :], x_sb[:, t, :])
                link(ins)
                for t in range(NT):
                    ins = dve.bn_aggr(mv[:, t, :], stats[:, t, :])
                link(ins)
                dve.tensor_scalar(rstd[:, :], mv[:, :, 1], LN_EPS, None, ALU.add).then_inc(s_var, 1)
                dve.wait_ge(s_std, n + 1)
                link(dve.reciprocal(rstd[:, :], std[:, :]))

                def normalise(t):
                    if n == 0 and t >= 2:
                        dve.wait_ge(s_xT, t - 1)
                    dve.tensor_scalar(xn_of(n, t), x_sb[:, t, :], mv[:, t, 0:1], rstd[:, t:t + 1],
                                      ALU.subtract, ALU.mult).then_inc(s_xn, 1)

                def low(t):
                    dve.wait_ge(s_xhi, NT * n + t + 1)
                    dve.scalar_tensor_tensor(
                        out=xT_lo[:, :, t * P:(t + 1) * P],
                        in0=ps[:, 5 + t % 2, :].rearrange("p (k m) -> p k m", k=KD), scalar=SX,
                        in1=xT_hi[:, :, t * P:(t + 1) * P], op0=ALU.mult, op1=ALU.subtract)\
                        .then_inc(s_xlo, 1)

                for t in range(NT):
                    normalise(t)
                    if t >= 1:
                        low(t - 1)
                low(NT - 1)

            dve.memset(x_sb[96:P, NT - 1, :], 0.0).then_inc(s_xpad, 1)
            E = slice(0, EP)
            dve.wait_ge(s_edges, 48)
            dve.wait_ge(s_const, 6)
            dve.tensor_scalar(edge_t[E, :, :], edge_in[E, 0:2, :], 7, None, ALU.logical_shift_right)
            link(dve.tensor_scalar(edge_l[E, :, :], edge_in[E, 0:2, :], P - 1, None, ALU.bitwise_and))
            dve.tensor_copy(tile_f[E, :, :], edge_t[E, :, :])
            dve.tensor_copy(place[E, :, :], edge_l[E, :, :])
            dve.tensor_copy(packed[E, 0, :, 0], edge_in[E, 1, :])
            dve.tensor_copy(packed[E, 1, :, 0], edge_in[E, 0, :])
            link(dve.tensor_copy(rel_f[E, :], edge_in[E, 2, :]))
            link(dve.tensor_scalar(rel_f[E, :], rel_f[E, :], 256.0, 1.0, ALU.mult, ALU.add))
            for l in range(2):
                dve.tensor_tensor(packed[E, l, :, 1], place[E, l, :], rel_f[E, :], ALU.add)
            for l in range(2):
                for b in range(NT):
                    ins = dve.tensor_scalar(in_bucket[E, l, b, :], tile_f[E, l, :], float(b), None, ALU.is_equal)
            link(ins)
            for l in range(2):
                for b in range(NT):
                    ins = dve.tensor_tensor_scan(running[E, l, b, :], ones[E, :], in_bucket[E, l, b, :], 0.0,
                                                 ALU.mult, ALU.add)
            link(ins)
            dve.tensor_copy(part_sum[E, :, :], running[E, :, :, EC - 1]).then_inc(s_sum, 1)
            layer_norm_part(0)
            split_lo(0, 0, 1)
            split_lo(1, 1, 2)
            dve.wait_ge(s_pre, 1)
            early = ps[:, 7, 0:2 * NT].rearrange("p (l b) -> p l b", l=2)
            total = ps[:, 7, 16:16 + 2 * NT].rearrange("p (l b) -> p l b", l=2)
            link(dve.tensor_scalar(pad_f[:, :, :], total, float(P - 1), None, ALU.add))
            link(dve.tensor_copy(pad_i[:, :, :], pad_f[:, :, :]))
            link(dve.tensor_scalar(pad_i[:, :, :], pad_i[:, :, :], -P, None, ALU.bitwise_and))
            link(dve.tensor_copy(pad_f[:, :, :], pad_i[:, :, :]))
            for l in range(2):
                ins = dve.tensor_tensor_scan(pad_end[:, l, :], ones[:, 0:NT], pad_f[:, l, :], 0.0, ALU.mult, ALU.add)
            link(ins)
            link(dve.tensor_tensor(pad_base[:, :, :], pad_end[:, :, :], pad_f[:, :, :], ALU.subtract))
            link(dve.scalar_tensor_tensor(out=offset[E, :, :], in0=pad_base[E, :, :], scalar=-1.0,
                                          in1=early[E, :, :], op0=ALU.add, op1=ALU.add))
            for l in range(2):
                for b in range(NT):
                    ins = dve.scalar_tensor_tensor(out=running[E, l, b, :], in0=running[E, l, b, :],
                                                   scalar=offset[E, l, b:b + 1], in1=in_bucket[E, l, b, :],
                                                   op0=ALU.add, op1=ALU.mult)
            link(ins)
            link(dve.tensor_tensor(place[E, :, :], running[E, :, 0, :], running[E, :, 1, :], ALU.add))
            for b in range(2, NT):
                link(dve.tensor_tensor(place[E, :, :], place[E, :, :], running[E, :, b, :], ALU.add))
            link(dve.tensor_copy(place_i[E, :, :], place[E, :, :]))
            dve.tensor_scalar(lo_i[E, :, :], place_i[E, :, :], P - 1, None, ALU.bitwise_and)
            link(dve.tensor_scalar(edge_t[E, :, :], place_i[E, :, :], 7, None, ALU.logical_shift_right))
            dve.tensor_copy(pos_lo[E, :], lo_i[E, :, :].rearrange("p l c -> p (l c)"))
            link(dve.tensor_copy(pos_hi[E, :], edge_t[E, :, :].rearrange("p l c -> p (l c)")))
            link(dve.tensor_scalar(pad_f[0:1, :, :], pad_base[0:1, :, :], 1.0 / P, None, ALU.mult))
            for l in range(2):
                link(dve.tensor_scalar(bank_f[:, l, :], iota_f[0:1, 0:EDGE_CHUNKS], pad_f[0:1, l, 1:2], None,
                                       ALU.is_ge))
                for b in range(2, NT):
                    link(dve.scalar_tensor_tensor(out=bank_f[:, l, :], in0=iota_f[0:1, 0:EDGE_CHUNKS],
                                                  scalar=pad_f[0:1, l, b:b + 1], in1=bank_f[:, l, :],
                                                  op0=ALU.is_ge, op1=ALU.add))
            dve.tensor_copy(bank_i[:, :, 0:EDGE_CHUNKS], bank_f[:, :, :]).then_inc(s_bank, 1)

            def sort_hots(r, t, first):
                if not first:
                    dve.wait_ge(s_sorted, COLS_PER_REL * r + COLS_PER_TILE * (t + 1) - COLS_PER_REL)
                for u in range(COLS_PER_TILE):
                    s = COLS_PER_TILE * t + u
                    col = bass.ds(COLS_PER_REL * r + s, 1)
                    dve.tensor_scalar(sort_hot[E, s, 0:P], iota_h[E, 0:P], pos_lo[E, col], None, ALU.is_equal)
                    dve.tensor_scalar(sort_hot[E, s, P:P + 2 * EDGE_CHUNKS].bitcast(F32), iota_f[E, 0:EDGE_CHUNKS],
                                      pos_hi[E, col], packed_pair[E, col], ALU.is_equal, ALU.mult)\
                        .then_inc(s_hot, 1)

            def dest_hots(l, j, slots):
                for n, s in enumerate(slots):
                    dve.tensor_scalar(dest_hot[:, s, :], iota_h[:, 0:P], dest_f[:, l, bass.ds(j + n, 1)], None,
                                      ALU.is_equal).then_inc(s_dhot, 1)

            def relation(r, q, first, second):
                for t in range(NT):
                    if t >= NT - 2:
                        slot = 2 * (1 - q) + t - (NT - 2)
                        split_lo(slot, slot, 2 * r + 3 + t - (NT - 2))
                    sort_hots(r, t, first)
                    if second is not None:
                        s0 = COLS_PER_REL * q + COLS_PER_TILE * t
                        if second > 0:
                            dve.wait_ge(s_seg, COLS_PER_REL * r + (COLS_PER_TILE * (t + 1) - RELS * COLS_PER_REL - SEG))
                        dest_hots(0, COLS_PER_REL * r + (COLS_PER_TILE * t - RELS * COLS_PER_REL),
                                  range(s0, s0 + COLS_PER_TILE))
                    dve.wait_ge(s_rhi, NT * r + t + 1)
                    dve.scalar_tensor_tensor(out=rows_out[:, q, t, D:2 * D], in0=ps[:, 5 + (q + t) % 2, :],
                                             scalar=SH / (SX * SW), in1=rows_out[:, q, t, 0:D],
                                             op0=ALU.mult, op1=ALU.subtract).then_inc(s_rlo, 1)

            def decode(l):
                dve.wait_ge(s_sorted, EC * (l + 1))
                node = ps[:, 7, 0:2 * EDGE_CHUNKS:2]
                code = ps[:, 7, 1:2 * EDGE_CHUNKS:2]
                link(dve.tensor_copy(code_i, code))
                dve.tensor_scalar(part_i[:, 0, :], code_i, 255, None, ALU.bitwise_and)
                link(dve.tensor_scalar(part_i[:, 1, :], code_i, 8, None, ALU.logical_shift_right))
                dve.tensor_scalar(dest_f[:, l, :], part_i[:, 0, :], -1.0, None, ALU.add)
                link(dve.tensor_scalar(row_rel, part_i[:, 1, :], float(PADDED), float(l * RELS * PADDED),
                                       ALU.mult, ALU.add))
                link(dve.tensor_tensor(row_rel, node, row_rel, ALU.add))
                for v in range(RELS):
                    dve.tensor_scalar(rel_hot[:, l, :, v], part_i[:, 1, :], float(v), None, ALU.is_equal)
                dve.tensor_copy(row_idx[:, l, :], row_rel).then_inc(s_dec, 1)

            relation(0, 0, True, None)
            relation(1, 1, False, None)
            with dve.Fori(1, RELS // 2) as i:
                relation(2 * i, 0, False, None)
                relation(2 * i + 1, 1, False, None)
            decode(0)
            half = RELS // 2
            relation(RELS, 0, False, 0)
            relation(RELS + 1, 1, False, 0)
            with dve.Fori(half + 1, RELS) as i:
                relation(2 * i, 0, False, 1)
                relation(2 * i + 1, 1, False, 1)
            dest_hots(0, EDGE_CHUNKS - 1, [SEG])
            dve.wait_ge(s_seg, EDGE_CHUNKS)
            decode(1)

            def hots_of_list1(i):
                for g in range(0, SEG, 4):
                    dve.wait_ge(s_seg, SEG * i + (EDGE_CHUNKS - SEG + g + 4))
                    dest_hots(1, SEG * i + g, range(g, g + 4))

            hots_of_list1(0)
            dve.wait_ge(s_tr, NT * (2 * RELS + 1))
            for j in range(KH):
                split_lo(j, j % RAW, GNN_CHUNKS + j + 1)
            dve.wait_ge(s_rwh, 1)
            dve.scalar_tensor_tensor(out=rw_lo[:, :], in0=rw_raw[:, :], scalar=SW, in1=rw_hi[:, :],
                                     op0=ALU.mult, op1=ALU.subtract).then_inc(s_rwl, 1)
            dve.tensor_scalar(b1_s[:, :], b1[:, :], SX * SW, None, ALU.mult)
            dve.wait_ge(s_self, NT)
            for t in range(NT):
                ins = dve.tensor_tensor(self_sb(t), self_sb(t), b_self_row[:, :], ALU.add)
            link(ins)
            dve.wait_ge(s_brel, 48)
            dve.memset(count, 0.0)
            link(dve.memset(b_parts, 0.0))
            for n in range(3):
                rows = slice(32 * n, 32 * n + 2 * RELS)
                ins = dve.tensor_scalar(b_parts[rows, :], b_rel_sb[rows, :], SH, None, ALU.mult)
            link(ins)
            rows = slice(32, 32 + 2 * RELS)
            dve.scalar_tensor_tensor(out=b_parts[rows, :], in0=b_rel_sb[rows, :], scalar=SH,
                                     in1=b_parts[rows, :], op0=ALU.mult, op1=ALU.subtract)
            with dve.Fori(1, 4) as i:
                hots_of_list1(i)
            dest_hots(1, EDGE_CHUNKS - 1, [SEG])

            dve.wait_ge(s_seg, 2 * EDGE_CHUNKS)
            counts = ps[:, 7, COUNTS:COUNTS + 2 * RELS * NT].rearrange("p (t r) -> p t r", t=NT)
            link(dve.tensor_copy(count_hi, counts))
            dve.tensor_copy(count[:, :, 0:2 * RELS], count_hi)
            dve.tensor_copy(count[:, :, 32:32 + 2 * RELS], count_hi)
            dve.tensor_tensor(count[:, :, 64:64 + 2 * RELS], counts, count_hi, ALU.subtract).then_inc(s_cnt, 1)
            dve.wait_ge(s_cntt, 1)
            dve.tensor_copy(countT[:, 0:4 * P], ps[0:BIAS_ROWS, 5, :])
            dve.tensor_copy(countT[:, 4 * P:], ps[0:BIAS_ROWS, 6, 0:P]).then_inc(s_cntc, 1)
            dve.wait_ge(s_bsum, 1)
            for t in range(NT):
                ins = dve.scalar_tensor_tensor(out=self_sb(t), in0=ps[:, t, :], scalar=1.0 / SH,
                                               in1=self_sb(t), op0=ALU.mult, op1=ALU.add)
            link(ins)
            for t in range(NT):
                ins = dve.scalar_tensor_tensor(out=x_sb[:, t, :], in0=self_sb(t), scalar=0.0,
                                               in1=x_sb[:, t, :], op0=ALU.max, op1=ALU.add)
            link(ins)
            layer_norm_part(1)

            dve.wait_ge(s_lg, 1)
            for t in range(NT):
                ins = dve.scalar_tensor_tensor(out=logits[:, t, :], in0=ps[:, 7, t * EXPERTS:(t + 1) * EXPERTS],
                                               scalar=1.0 / (SX * SW), in1=rb_row[:, :],
                                               op0=ALU.mult, op1=ALU.add)
            link(ins)
            for t in range(NT):
                ins = dve.max(top[:, t, :], logits[:, t, :])
            link(ins)
            for t in range(NT):
                ins = dve.max_index(top_i[:, t, :], top[:, t, :], logits[:, t, :])
            dve.tensor_tensor(soft[:, 0, :], top[:, :, 1], top[:, :, 0], ALU.subtract).then_inc(s_dif, 1)
            link(ins)
            link(dve.tensor_copy(top_if[:, :, :], top_i[:, :, :]))
            for e in range(EXPERTS):
                dve.scalar_tensor_tensor(out=hot1[:, :, e], in0=top_if[:, :, 0], scalar=float(e),
                                         in1=valid[:, :], op0=ALU.is_equal, op1=ALU.mult)
                ins = dve.scalar_tensor_tensor(out=hot2[:, :, e], in0=top_if[:, :, 1], scalar=float(e),
                                               in1=valid[:, :], op0=ALU.is_equal, op1=ALU.mult)
            link(ins)
            link(dve.tensor_tensor(mask[:, :, :], hot1[:, :, :], hot2[:, :, :], ALU.add))
            link(dve.tensor_copy(cum[:, 0, :], mask[:, 0, :]))
            for t in range(1, NT):
                link(dve.tensor_tensor(cum[:, t, :], cum[:, t - 1, :], mask[:, t, :], ALU.add))
            dve.sem_inc(s_cum, 1)
            def by_tile(a):
                return a.rearrange("p (t a) -> p t a", a=1).to_broadcast([P, NT, EXPERTS])

            def by_expert(a):
                return a.rearrange("p (a e) -> p a e", a=1).to_broadcast([P, NT, EXPERTS])

            dve.wait_ge(s_epre, 1)
            early = ps[:, 7, 0:EXPERTS]
            total = ps[:, 7, 16:16 + EXPERTS]
            link(dve.tensor_scalar(np_f[:, :], total, float(P - 1), None, ALU.add))
            link(dve.tensor_copy(np_i[:, :], np_f[:, :]))
            link(dve.tensor_scalar(np_i[:, :], np_i[:, :], 7, None, ALU.logical_shift_right))
            link(dve.tensor_copy(end_f[:, :], np_i[:, :]))
            link(dve.tensor_scalar(np_f[:, :], end_f[:, :], 1.0, None, ALU.max))
            link(dve.tensor_tensor_scan(end_f[:, :], ones[:, 0:EXPERTS], np_f[:, :], 0.0, ALU.mult, ALU.add))
            dve.tensor_copy(plan_i[:, :, 1], np_f[0:1, :])
            link(dve.tensor_tensor(first_f[:, :], end_f[:, :], np_f[:, :], ALU.subtract))
            dve.tensor_copy(plan_i[:, :, 0], first_f[0:1, :])
            link(dve.tensor_tensor(pos[:, :, :], cum[:, :, :], mask[:, :, :], ALU.subtract))
            link(dve.tensor_tensor(pos[:, :, :], pos[:, :, :], by_expert(early), ALU.add))
            link(dve.scalar_tensor_tensor(out=cum[:, :, :], in0=pos[:, :, :], scalar=1.0, in1=mask[:, :, :],
                                          op0=ALU.add, op1=ALU.mult))
            for c in range(NT + 1):
                ins = dve.tensor_scalar(in_pass[:, c, :, :], cum[:, :, :].rearrange("p t e -> p e t"),
                                        -1.0 - P * c, None, ALU.add)
            link(ins)
            dve.sem_inc(s_plan, 1)
            for t in range(NT):
                ins = dve.tensor_scalar(main_hot[0][:, t, :], iota_h[:, 0:P], in_pass[:, 0, 0, t:t + 1], None,
                                        ALU.is_equal)
            ins.then_inc(s_mslot, 1)

            def rows_of_tokens():
                link(dve.tensor_scalar(np_f[:, :], first_f[:, :], float(P), None, ALU.mult))
                link(dve.tensor_tensor(pos[:, :, :], pos[:, :, :], by_expert(np_f[:, :]), ALU.add))
                link(dve.tensor_tensor(hot1[:, :, :], hot1[:, :, :], pos[:, :, :], ALU.mult))
                link(dve.tensor_tensor(hot2[:, :, :], hot2[:, :, :], pos[:, :, :], ALU.mult))
                dve.tensor_reduce(y_row[:, 0, :], hot1[:, :, :], AX_X, ALU.add)
                link(dve.tensor_reduce(y_row[:, 1, :], hot2[:, :, :], AX_X, ALU.add))
                link(dve.tensor_copy(y_idx[:, :, :], y_row[:, :, :]))

            def expert(e, parity, last):
                def one(e, c, q, main):
                    splits = chunks_in_pass(e, parity, last, main)
                    for g, tiles in enumerate(GROUPS):
                        for chunk in splits[g]:
                            split_ffn(*chunk)
                        for at, j in enumerate(tiles):
                            dve.wait_ge(s_silu, KH * q + j + 1)
                            ins = dve.scalar_tensor_tensor(
                                out=glu[:, j, :], in0=ps[:, GROUP_BANKS[g][1], at * P:(at + 1) * P],
                                scalar=b1_s[:, bass.ds(2 * KH * e + KH + j, 1)], in1=silu[:, j, :],
                                op0=ALU.add, op1=ALU.mult)
                        ins.then_inc(s_glu, 1)
                        dve.wait_ge(s_ahi, len(GROUPS) * q + g + 1)
                        dve.scalar_tensor_tensor(
                            out=aT_lo[:, tiles[0]:tiles[-1] + 1, :], in0=glu[:, tiles[0]:tiles[-1] + 1, :],
                            scalar=SA / (SX * SW), in1=aT_hi[:, tiles[0]:tiles[-1] + 1, :],
                            op0=ALU.mult, op1=ALU.subtract).then_inc(s_alo, 1)
                    for chunk in splits[-2] + splits[-1]:
                        split_ffn(*chunk)

                passes(dve, mybir.EngineType.DVE, e, one)

            def split_ffn(e, n, parity):
                split_lo(n, n % RAW, SLOTS * e + (GNN_CHUNKS + n + 1), *wset[parity])

            dve.wait_ge(s_exp, 1)
            link(dve.tensor_scalar(soft[:, 0, :], soft[:, 1, :], 1.0, None, ALU.add))
            link(dve.reciprocal(soft[:, 2, :], soft[:, 0, :]))
            link(dve.tensor_tensor(soft[:, 3, :], soft[:, 1, :], soft[:, 2, :], ALU.mult))
            dve.tensor_tensor(cw_a[:, :, :], hot1[:, :, :], by_tile(soft[:, 2, :]), ALU.mult)
            link(dve.tensor_tensor(cw[:, :, :], hot2[:, :, :], by_tile(soft[:, 3, :]), ALU.mult))
            dve.tensor_tensor(cw[:, :, :], cw[:, :, :], cw_a[:, :, :], ALU.add).then_inc(s_cw, 1)
            rows_of_tokens()
            pairs(dve, expert)
            dve.wait_ge(s_cwt, 1)
            dve.tensor_copy(cwT[:, 0:4 * P], ps[0:EXPERTS, 0, :])
            dve.tensor_copy(cwT[:, 4 * P:], ps[0:EXPERTS, 1, 0:P]).then_inc(s_cwc, 1)
            for t in range(NT):
                dve.wait_ge(s_b2, t + 1)
                dve.tensor_tensor(acc[:, t, :], ps[:, BIAS2_BANKS[t], :], x_sb[:, t, :], ALU.add).then_inc(s_acc, 1)
            for t in range(NT):
                dve.wait_ge(s_acc, t + 1)
                dve.wait_ge(s_ygat[t], 32)
                for n in range(2):
                    ins = dve.scalar_tensor_tensor(out=acc[:, t, :], in0=w_raw[:, t % GNN_RAW, n * D:(n + 1) * D],
                                                   scalar=soft[:, 2 + n, t:t + 1], in1=acc[:, t, :],
                                                   op0=ALU.mult, op1=ALU.add)
                    if n == 0:
                        ins.then_inc(s_half, 1)
                        dve.wait_ge(s_half, t + 1)
                ins.then_inc(s_done, 1)

        @block.tensor
        def _(pe):
            def product(to, lhs, rhs, terms, skip=False):
                n = 0
                for k in terms:
                    (lh, ll), (rh, rl) = lhs(k), rhs(k)
                    for a, b in ((lh, rh), (lh, rl), (ll, rh)):
                        ins = pe.matmul(to, a, b, start=(n == 0), stop=(n == 3 * len(terms) - 1))
                        n += 1
                return ins

            def layer_norm_part(n):
                for t in range(NT):
                    pe.wait_ge(s_xn, NT * n + t + 1)
                    if t >= 2:
                        pe.wait_ge(s_xlo, NT * n + t - 1)
                    for k in range(KD):
                        ins = pe.transpose(ps[:, 5 + t % 2, k * P:(k + 1) * P], xn_of(n, t)[:, k * P:(k + 1) * P],
                                           ident[:, :])
                    ins.then_inc(s_xT, 1)

            pe.wait_ge(s_const, 5)
            pe.wait_ge(s_sum, 1)
            pe.matmul(ps[:, 7, 0:2 * NT], before[0:EP, :], part_sum[0:EP, :, :].rearrange("p l b -> p (l b)"),
                      start=True, stop=True)
            pe.matmul(ps[:, 7, 16:16 + 2 * NT], ones[0:EP, 0:P], part_sum[0:EP, :, :].rearrange("p l b -> p (l b)"),
                      start=True, stop=True).then_inc(s_pre, 1)
            layer_norm_part(0)

            def sum_chunk(slot, hot, of, n_gathered, n_hot):
                pe.wait_ge(s_gat[slot], n_gathered)
                pe.wait_ge(s_dhot, n_hot)
                l, j, tile = of
                for part_at in range(2):
                    pe.matmul(ps_flat[:, bass.ds(tile * D, D)], dest_hot[:, hot, :],
                              gathered[:, slot, part_at * D:(part_at + 1) * D], start=False, stop=True,
                              skip_group_check=True)
                pe.matmul(ps_flat[:, bass.ds(tile * (2 * RELS) + (7 * 512 + COUNTS + RELS * l), RELS)],
                          dest_hot[:, hot, :], rel_hot[:, l, bass.ds(j, 1), :].rearrange("p a r -> p (a r)"),
                          start=False, stop=True, skip_group_check=True).then_inc(s_seg, 1)

            def tiles_of(l, j, n):
                _, tiles = nc.values_load_multi_w_load_instructions(
                    bank_i[0:1, l, bass.ds(j, n)], engines=[mybir.EngineType.PE], min_val=0, max_val=NT - 1)
                return [(l, j + u, tile) for u, tile in enumerate(tiles)]

            def relation(r, q, first, second, i=None):
                def transform(t):
                    if t == 0:
                        pe.wait_ge(s_wlo, 2 * r + 2)
                    if first and t < 2:
                        pe.wait_ge(s_xlo, NT)
                    else:
                        pe.wait_ge(s_rlo, NT * r + t - 1)
                    w = lambda k: 2 * q + k // 2
                    product(ps[:, 5 + (q + t) % 2, :],
                            lambda k: (xT_hi[:, k, t * P:(t + 1) * P], xT_lo[:, k, t * P:(t + 1) * P]),
                            lambda k: (w_hi[:, w(k), (k % 2) * D:(k % 2 + 1) * D],
                                       w_lo[:, w(k), (k % 2) * D:(k % 2 + 1) * D]),
                            range(KD)).then_inc(s_tr, 1)

                def sort_columns(t):
                    for u in range(COLS_PER_TILE):
                        s = COLS_PER_TILE * t + u
                        pe.wait_ge(s_hot, COLS_PER_REL * r + s + 1)
                        pe.matmul(ps[:, 7, 0:2 * EDGE_CHUNKS], sort_hot[0:EP, s, 0:P],
                                  sort_hot[0:EP, s, P:P + 2 * EDGE_CHUNKS],
                                  start=False, stop=True, skip_group_check=True).then_inc(s_sorted, 1)

                if first:
                    transform(0)
                    transform(1)
                    pe.wait_ge(s_bank, 1)
                    pe.matmul(ps[:, 7, :], zeros[:, 0:P], zeros[:, :], start=True, stop=True)
                for t in range(NT):
                    if not first or t >= 2:
                        transform(t)
                    sort_columns(t)
                    if second:
                        first_chunk = COLS_PER_REL * r + (COLS_PER_TILE * t - RELS * COLS_PER_REL)
                        s0 = COLS_PER_REL * q + COLS_PER_TILE * t
                        for u, of in enumerate(tiles_of(0, first_chunk, COLS_PER_TILE)):
                            sum_chunk((s0 + u) % RING, s0 + u, of,
                                      32 * i + 16 * (q - RELS + 1), first_chunk + u + 1)

            relation(0, 0, True, False)
            relation(1, 1, False, False)
            with pe.Fori(1, RELS // 2) as i:
                relation(2 * i, 0, False, False)
                relation(2 * i + 1, 1, False, False)
            pe.wait_ge(s_dec, 1)
            for t in (*range(NT), 7):
                pe.matmul(ps[:, t, :], zeros[:, 0:P], zeros[:, :], start=True, stop=True)
            half = RELS // 2
            relation(RELS, 0, False, True, half)
            relation(RELS + 1, 1, False, True, half)
            with pe.Fori(half + 1, RELS) as i:
                relation(2 * i, 0, False, True, i)
                relation(2 * i + 1, 1, False, True, i)
            sum_chunk(RING, SEG, tiles_of(0, EDGE_CHUNKS - 1, 1)[0], 16, EDGE_CHUNKS)
            pe.wait_ge(s_wlo, GNN_CHUNKS)
            for t in range(NT):
                if t < 2:
                    pe.wait_ge(s_rlo, 2 * RELS * NT)
                else:
                    pe.wait_ge(s_self, t - 1)
                product(ps[:, 5 + t % 2, :],
                        lambda k: (xT_hi[:, k, t * P:(t + 1) * P], xT_lo[:, k, t * P:(t + 1) * P]),
                        lambda k: (w_hi[:, k // 2, (k % 2) * D:(k % 2 + 1) * D],
                                   w_lo[:, k // 2, (k % 2) * D:(k % 2 + 1) * D]),
                        range(KD)).then_inc(s_tr, 1)
            turns = EDGE_CHUNKS // RING
            with pe.Fori(0, 4) as i:
                for g in range(0, SEG, 4):
                    for s, of in enumerate(tiles_of(1, SEG * i + g, 4), g):
                        sum_chunk(s % RING, s, of, 32 * i + 16 * (turns + s // RING + 1),
                                  SEG * i + (EDGE_CHUNKS + s + 1))
            sum_chunk(RING, SEG, tiles_of(1, EDGE_CHUNKS - 1, 1)[0], 32, 2 * EDGE_CHUNKS)

            pe.wait_ge(s_self, NT)
            pe.wait_ge(s_cnt, 1)
            for t in range(NT):
                to = ps[0:BIAS_ROWS, 5, t * P:(t + 1) * P] if t < 4 else ps[0:BIAS_ROWS, 6, 0:P]
                ins = pe.transpose(to, count[:, t, :], ident[:, :])
            ins.then_inc(s_cntt, 1)
            pe.wait_ge(s_cntc, 1)
            for t in range(NT):
                ins = pe.matmul(ps[:, t, :], countT[:, t * P:(t + 1) * P], b_parts, start=False, stop=True,
                                skip_group_check=True)
            ins.then_inc(s_bsum, 1)
            layer_norm_part(1)
            pe.wait_ge(s_xlo, 2 * NT)
            pe.wait_ge(s_rwl, 1)
            pe.wait_ge(s_dec, 2)
            for t in range(NT):
                ins = product(ps[:, 7, t * EXPERTS:(t + 1) * EXPERTS],
                              lambda k: (xT_hi[:, k, t * P:(t + 1) * P], xT_lo[:, k, t * P:(t + 1) * P]),
                              lambda k: (rw_hi[:, k * EXPERTS:(k + 1) * EXPERTS],
                                         rw_lo[:, k * EXPERTS:(k + 1) * EXPERTS]),
                              range(KD))
            ins.then_inc(s_lg, 1)
            pe.wait_ge(s_cum, 1)
            pe.matmul(ps[:, 7, 0:EXPERTS], before[:, :], cum[:, NT - 1, :], start=True, stop=True)
            pe.matmul(ps[:, 7, 16:16 + EXPERTS], ones[:, 0:P], cum[:, NT - 1, :], start=True, stop=True)\
                .then_inc(s_epre, 1)
            pe.wait_ge(s_xrl, NT)
            pe.wait_ge(s_plan, 1)
            pe.sem_inc(s_disp, 1)

            def expert(e, parity):
                wh, wl = wset[parity]

                def one(e, c, q, main):
                    if main:
                        pe.wait_ge(s_mslot, e + 1)
                    else:
                        pe.wait_ge(s_slot, q)
                    hot = main_hot[parity] if main else slot_hot
                    for n, rows in enumerate((xr_hi, xr_lo)):
                        for k in range(KD):
                            for t in range(NT):
                                ins = pe.matmul(ps[:, n, k * P:(k + 1) * P], rows[:, t, k * P:(k + 1) * P],
                                                hot[:, t, :], start=(t == 0), stop=(t == NT - 1))
                        ins.then_inc(s_disp if n else s_disph, 1)
                    pe.wait_ge(s_xgh, q + 1)

                    def fc1(at, half, first, second):
                        g, j = at
                        to = GROUPS[g].index(j) * P
                        to = ps[:, GROUP_BANKS[g][half], to:to + P]
                        for k in range(KD):
                            w_h, w_l = (w[:, j, (2 * k + half) * P:(2 * k + half + 1) * P] for w in (wh, wl))
                            for n, w in enumerate((w_h, w_l) if first else ()):
                                pe.matmul(to, w, xg_hi[:, k, :], start=(k == 0 and n == 0), stop=False)
                        for k in range(KD if second else 0):
                            w_h = wh[:, j, (2 * k + half) * P:(2 * k + half + 1) * P]
                            ins = pe.matmul(to, w_h, xg_lo[:, k, :], start=False, stop=(k == KD - 1))
                        return ins if second else None

                    for g, tiles in enumerate(GROUPS):
                        for j in tiles:
                            if main:
                                pe.wait_ge(s_wlo, SLOTS * e + (GNN_CHUNKS + j + 1))
                            if j == 0:
                                fc1((g, j), 0, True, False)
                                fc1((g, j), 1, True, False)
                                pe.wait_ge(s_xgl, q + 1)
                            for half in range(2):
                                ins = fc1((g, j), half, j > 0, True)
                        ins.then_inc(s_fc1, 1)
                    pe.wait_ge(s_y, q + 1)
                    for g, tiles in enumerate(GROUPS):
                        pe.wait_ge(s_alo, len(GROUPS) * q + g + 1)
                        for k in tiles:
                            if main and k % 2 == 0:
                                pe.wait_ge(s_wlo, SLOTS * e + (GNN_CHUNKS + KH + k // 2 + 1))
                            w_h, w_l = (w[:, KH + k // 2, (k % 2) * D:(k % 2 + 1) * D] for w in (wh, wl))
                            for n, (a, b) in enumerate(((aT_hi, w_h), (aT_hi, w_l), (aT_lo, w_h))):
                                ins = pe.matmul(ps[:, 6, :], a[:, k, :], b, start=(k == 0 and n == 0),
                                                stop=(k == KH - 1 and n == 2))
                    ins.then_inc(s_fc2, 1)

                passes(pe, mybir.EngineType.PE, e, one)

            with pe.Fori(0, EXPERTS // 2) as i:
                expert(2 * i, 0)
                expert(2 * i + 1, 1)
            pe.wait_ge(s_cw, 1)
            for t in range(NT):
                ins = pe.transpose(ps[0:EXPERTS, t // 4, (t % 4) * P:(t % 4 + 1) * P], cw[:, t, :], ident[:, :])
            ins.then_inc(s_cwt, 1)
            pe.wait_ge(s_cwc, 1)
            for t in range(NT):
                pe.matmul(ps[:, BIAS2_BANKS[t], :], cwT[:, t * P:(t + 1) * P], b2[:, :], start=True, stop=True)\
                    .then_inc(s_b2, 1)


def kernel(x, src, dst, edge_type_8, L0_gnn_W_self, L0_gnn_b_self, L0_gnn_W_rel, L0_gnn_b_rel,
           L0_ffn_router_w, L0_ffn_router_b, L0_ffn_fc1_w, L0_ffn_fc1_b, L0_ffn_fc2_w, L0_ffn_fc2_b):
    import numpy as np
    import concourse.bacc as bacc
    from concourse.bass_utils import run_bass_kernel_spmd

    gnn = np.concatenate([np.asarray(L0_gnn_W_rel), np.asarray(L0_gnn_W_self)[None]])
    gnn = gnn.transpose(0, 2, 1).reshape(2 * RELS + 1, 2, 2, P, D).transpose(0, 1, 3, 2, 4)
    gnn = gnn.reshape(GNN_CHUNKS, P, CH)
    fc1 = np.asarray(L0_ffn_fc1_w).reshape(EXPERTS, 2, KH, P, KD, P).transpose(0, 2, 5, 4, 1, 3)
    fc1 = fc1.reshape(EXPERTS, KH, P, CH)
    fc2 = np.asarray(L0_ffn_fc2_w).transpose(0, 2, 1).reshape(EXPERTS, 4, 2, P, D).transpose(0, 1, 3, 2, 4)
    fc2 = fc2.reshape(EXPERTS, 4, P, CH)
    named = {
        "x": x, "src": src, "dst": dst, "rel": edge_type_8, "gnn_w": gnn,
        "b_self": np.asarray(L0_gnn_b_self)[None], "b_rel": L0_gnn_b_rel,
        "router_w": np.asarray(L0_ffn_router_w).reshape(EXPERTS, KD, P).transpose(2, 1, 0).reshape(P, KD * EXPERTS),
        "router_b": np.asarray(L0_ffn_router_b)[None],
        "ffn_w": np.concatenate([fc1, fc2], axis=1).reshape(EXPERTS * SLOTS, P, CH),
        "fc1_b": np.asarray(L0_ffn_fc1_b).reshape(EXPERTS * 2 * KH, P).transpose(1, 0),
        "fc2_b": L0_ffn_fc2_b,
    }
    nc = bacc.Bacc("TRN2", target_bir_lowering=False, num_devices=1)
    arrays, args = {}, []
    for name, a in named.items():
        a = np.ascontiguousarray(a)
        arrays[f"in_{name}"] = a
        args.append(nc.dram_tensor(f"in_{name}", a.shape, mybir.dt.from_np(a.dtype), kind="ExternalInput").ap())
    args.append(nc.dram_tensor("out_x", (NODES, D), F32, kind="ExternalOutput").ap())
    build(nc, *args)
    return run_bass_kernel_spmd(nc, [arrays], core_ids=[0]).results[0]["out_x"]
```
